# Optimizing a Trainium2 kernel written in Bass

```python
import numpy as np
import jax
import jax.numpy as jnp

def _softmax(x, axis=-1):
    return jax.nn.softmax(x, axis=axis)

def _gelu(x):
    return jax.nn.gelu(x, approximate=True)

def _silu(x):
    return jax.nn.silu(x)

def _sigmoid(x):
    return jax.nn.sigmoid(x)

def _layernorm(x, axis=-1, eps=1e-05):
    m = jnp.mean(x, axis=axis, keepdims=True)
    v = jnp.var(x, axis=axis, keepdims=True)
    return (x - m) / jnp.sqrt(v + eps)

def _scatter_add(tgt, idx, src, axis=0):
    return tgt.at[idx].add(src)

def _segment_sum(src, seg, n):
    return jax.ops.segment_sum(src, seg, n)
kernel_name = 'mk_conv_attn_hybrid_d2_conv_nhwc256_r4_7f434f'

def setup_inputs(seed: int=0):
    np.random.seed(seed)
    _w = jnp.asarray

    def _rec_inputs():
        import jax
        import jax.numpy as jnp
        _gk = jax.random.key(seed)
        x = -0.0002928 + 1 * jax.random.normal(jax.random.fold_in(_gk, 1), (4, 16, 16, 64), jnp.float32)
        return x
    x = _rec_inputs()

    def _L0_conv_setup():
        import jax, jax.numpy as jnp
        import numpy as np
        FILTERS = 64
        QK_DIM = FILTERS // 8
        key = jax.random.key(seed)
        ks = jax.random.split(key, 8)
        B, H, W, C = (4, 16, 16, FILTERS)
        x = jax.random.normal(ks[0], (B, H, W, C), dtype=jnp.float32)
        wq = jax.random.normal(ks[1], (C, QK_DIM), dtype=jnp.float32) * 0.05
        bq = jnp.zeros((QK_DIM,), dtype=jnp.float32)
        wk = jax.random.normal(ks[2], (C, QK_DIM), dtype=jnp.float32) * 0.05
        bk = jnp.zeros((QK_DIM,), dtype=jnp.float32)
        wv = jax.random.normal(ks[3], (C, C), dtype=jnp.float32) * 0.05
        bv = jnp.zeros((C,), dtype=jnp.float32)
        gamma = jnp.asarray(0.5, dtype=jnp.float32)
        return {'x': x, 'wq': wq, 'bq': bq, 'wk': wk, 'bk': bk, 'wv': wv, 'bv': bv, 'gamma': gamma}
    _L0_conv_all = _L0_conv_setup()
    _L0_conv_in = {k: v for k, v in _L0_conv_all.items() if k in ('wq', 'bq', 'wk', 'bk', 'wv', 'bv', 'gamma')}
    del _L0_conv_all

    def _L1_attn_setup():
        import jax, jax.numpy as jnp
        import numpy as np
        key = jax.random.key(seed)
        k1, k2, k3 = jax.random.split(key, 3)
        b, n_t, n, n_h = (8, 256, 64, 8)
        s = jax.random.normal(k1, (b, n_t, n), dtype=jnp.float32)
        Q = jax.random.normal(k2, (n_h, n, n), dtype=jnp.float32) * 0.02
        E = jax.random.normal(k3, (n_h, n, n), dtype=jnp.float32) * 0.02
        return {'s': s, 'Q': Q, 'E': E}
    _L1_attn_all = _L1_attn_setup()
    _L1_attn_in = {k: v for k, v in _L1_attn_all.items() if k in ('Q', 'E')}
    del _L1_attn_all

    def _L1_ffn_setup():
        import jax, jax.numpy as jnp
        import numpy as np
        D_MODEL = 64
        N_EXPERTS = 16
        HIDDEN = 128
        SCALE = 0.02
        key = jax.random.key(seed)
        ks = jax.random.split(key, 5)
        x = jax.random.normal(ks[0], (4, 2048, D_MODEL), dtype=jnp.float32)
        gate_w = jax.random.normal(ks[1], (D_MODEL, N_EXPERTS), dtype=jnp.float32) * SCALE
        gate_b = jnp.zeros((N_EXPERTS,), dtype=jnp.float32)
        w1 = jax.random.normal(ks[2], (N_EXPERTS, D_MODEL, HIDDEN), dtype=jnp.float32) * SCALE
        w2 = jax.random.normal(ks[3], (N_EXPERTS, D_MODEL, HIDDEN), dtype=jnp.float32) * SCALE
        w3 = jax.random.normal(ks[4], (N_EXPERTS, HIDDEN, D_MODEL), dtype=jnp.float32) * SCALE
        return {'x': x, 'gate_w': gate_w, 'gate_b': gate_b, 'w1': w1, 'w2': w2, 'w3': w3}
    _L1_ffn_all = _L1_ffn_setup()
    _L1_ffn_in = {k: v for k, v in _L1_ffn_all.items() if k in ('gate_w', 'gate_b', 'w1', 'w2', 'w3')}
    del _L1_ffn_all
    return {'x': x, 'L0_conv_wq': _L0_conv_in['wq'], 'L0_conv_bq': _L0_conv_in['bq'], 'L0_conv_wk': _L0_conv_in['wk'], 'L0_conv_bk': _L0_conv_in['bk'], 'L0_conv_wv': _L0_conv_in['wv'], 'L0_conv_bv': _L0_conv_in['bv'], 'L0_conv_gamma': _L0_conv_in['gamma'], 'L1_attn_Q': _L1_attn_in['Q'], 'L1_attn_E': _L1_attn_in['E'], 'L1_ffn_gate_w': _L1_ffn_in['gate_w'], 'L1_ffn_gate_b': _L1_ffn_in['gate_b'], 'L1_ffn_w1': _L1_ffn_in['w1'], 'L1_ffn_w2': _L1_ffn_in['w2'], 'L1_ffn_w3': _L1_ffn_in['w3']}

def reference(x, L0_conv_wq, L0_conv_bq, L0_conv_wk, L0_conv_bk, L0_conv_wv, L0_conv_bv, L0_conv_gamma, L1_attn_Q, L1_attn_E, L1_ffn_gate_w, L1_ffn_gate_b, L1_ffn_w1, L1_ffn_w2, L1_ffn_w3):
    import jax
    import jax.numpy as jnp

    def _L0_conv_ref(x, wq, bq, wk, bk, wv, bv, gamma):
        import jax, jax.numpy as jnp
        import numpy as np
        FILTERS = 64
        QK_DIM = FILTERS // 8
        B, H, W, C = x.shape
        N = H * W
        xf = x.reshape(B, N, C)
        q = xf @ wq + bq
        k = xf @ wk + bk
        v = xf @ wv + bv
        attn = jax.nn.softmax(jnp.einsum('bnd,bmd->bnm', q, k), axis=-1)
        out = jnp.einsum('bnm,bmc->bnc', attn, v).reshape(B, H, W, C)
        return gamma * out + x

    def _L1_attn_ref(s, Q, E):
        import jax, jax.numpy as jnp
        import numpy as np
        n_t = s.shape[1]
        qs = jnp.einsum('bti,hij->bhtj', s, Q)
        Omega = jnp.einsum('bhtj,buj->bhtu', qs, s)
        mask = jnp.tril(jnp.ones((n_t, n_t), dtype=s.dtype))
        Omega = Omega * mask
        es = jnp.einsum('hij,buj->bhui', E, s)
        r = jnp.einsum('bhtu,bhui->bti', Omega, es)
        return r

    def _L1_ffn_ref(x, gate_w, gate_b, w1, w2, w3):
        import jax, jax.numpy as jnp
        import numpy as np
        D_MODEL = 64
        N_EXPERTS = 16
        HIDDEN = 128
        SCALE = 0.02
        n_experts = w1.shape[0]
        logits = jnp.einsum('bsd,de->bse', x, gate_w) + gate_b
        probs = jax.nn.softmax(logits, axis=-1)
        top_probs, top_idx = jax.lax.top_k(probs, 2)
        top_probs = top_probs / jnp.sum(top_probs, axis=-1, keepdims=True)
        dispatch = jnp.sum(jax.nn.one_hot(top_idx, n_experts, dtype=x.dtype) * top_probs[..., None], axis=-2)
        h1 = jnp.einsum('bsd,edh->bseh', x, w1)
        h2 = jnp.einsum('bsd,edh->bseh', x, w2)
        hidden = jax.nn.silu(h1) * h2
        expert_out = jnp.einsum('bseh,eho->bseo', hidden, w3)
        return jnp.einsum('bseo,bse->bso', expert_out, dispatch)

    def _gn(v, G=32, eps=1e-05):
        B_, H_, W_, C_ = v.shape
        g = v.reshape(B_, H_, W_, G, C_ // G)
        m = jnp.mean(g, axis=(1, 2, 4), keepdims=True)
        s = jnp.var(g, axis=(1, 2, 4), keepdims=True)
        return ((g - m) / jnp.sqrt(s + eps)).reshape(v.shape)

    def _ln_c(v, eps=1e-06):
        m = jnp.mean(v, axis=-1, keepdims=True)
        s = jnp.var(v, axis=-1, keepdims=True)
        return (v - m) / jnp.sqrt(s + eps)

    def _ln_t(v, eps=1e-05):
        m = jnp.mean(v, axis=-1, keepdims=True)
        s = jnp.var(v, axis=-1, keepdims=True)
        return (v - m) / jnp.sqrt(s + eps)

    def _to_tokens(v):
        B_, H_, W_, C_ = v.shape
        return v.reshape(B_, H_ * W_, C_)

    def _from_tokens(t, like):
        return t.reshape(like.shape)
    x = _L0_conv_ref(x, L0_conv_wq, L0_conv_bq, L0_conv_wk, L0_conv_bk, L0_conv_wv, L0_conv_bv, L0_conv_gamma)
    t = _to_tokens(x)
    t = t + _L1_attn_ref(_ln_t(t), L1_attn_Q, L1_attn_E)
    t = t + _L1_ffn_ref(_ln_t(t), L1_ffn_gate_w, L1_ffn_gate_b, L1_ffn_w1, L1_ffn_w2, L1_ffn_w3)
    x = _from_tokens(t, x)
    return x

_drawn_inputs = setup_inputs


def setup_inputs(seed=0):
    import zlib

    import numpy as np

    out = dict(_drawn_inputs(seed))
    spreads = {'L0_conv_bq': (0.0, 0.8),
     'L0_conv_bk': (0.0, 0.8),
     'L0_conv_bv': (0.0, 0.1),
     'L1_ffn_gate_b': (0.0, 0.8)}
    factors = {'L0_conv_wq': 2.683,
     'L1_ffn_gate_w': 8.0,
     'L1_ffn_w1': 8.0,
     'L1_ffn_w2': 8.0,
     'L1_ffn_w3': 8.0}
    for name, (base, spread) in spreads.items():
        noise = np.random.default_rng([zlib.crc32(name.encode()), seed]).standard_normal(out[name].shape)
        drawn = base * np.exp(spread * noise) if base else spread * noise
        out[name] = jnp.asarray(drawn.astype(out[name].dtype))
    for name, factor in factors.items():
        out[name] = (out[name] * factor).astype(out[name].dtype)
    return out
```

```python
import concourse.bass as bass
from concourse import mybir
from contextlib import ExitStack

FP32 = mybir.dt.float32
F32R = mybir.dt.float32r
ALU = mybir.AluOpType
ACT = mybir.ActivationFunctionType
AX = mybir.AxisListType

P = 128
IMAGES = 4
TOKENS = 256
TILES = TOKENS // P
C = 64
QK = 8
HEADS = 8
PAIRS = HEADS // 2
EXPERTS = 16
HIDDEN = 128
HALVES = 2
HALF = IMAGES * TOKENS // HALVES
HTILES = HALF // P
UNITS = HALVES * EXPERTS
LAG = 4
SIL, UU, HID = 3, 4, 6

SCHEDULE = (
    [("A", 0), ("B", 0), ("X", 0), ("V", 0), ("A", 1), ("C", 0), ("B", 1), ("V", 1), ("D", 0), ("C", 1), ("E", 0),
     ("A", 2), ("F", 0), ("D", 1), ("H", 0), ("E", 1), ("B", 2),
     ("P", 0), ("V", 2), ("F", 1), ("C", 2), ("P", 1), ("A", 3), ("W", 0), ("D", 2), ("P", 2), ("H", 1), ("B", 3), ("E", 2), ("W", 1),
     ("P", 3), ("V", 3), ("F", 2), ("P", 4), ("C", 3), ("N", 0), ("W", 2), ("P", 5), ("D", 3), ("R", 0), ("H", 2), ("W", 3),
     ("P", 6), ("E", 3), ("G", 0), ("P", 7), ("W", 4), ("F", 3),
     ("P", 8), ("N", 1), ("P", 9), ("R", 1), ("W", 5), ("P", 10), ("H", 3), ("G", 1), ("W", 6), ("P", 11), ("L", 0),
     ("P", 12), ("N", 2), ("M", 0), ("W", 7), ("P", 13), ("R", 2), ("T", 0), ("P", 14), ("G", 2), ("P", 15),
     ("P", 16), ("N", 3), ("U", 0), ("R", 3), ("U", 1), ("G", 3), ("U", 2), ("U", 3), ("L", 1), ("U", 4), ("M", 1),
     ("U", 5), ("T", 1)]
    + [("U", n) for n in range(6, EXPERTS + LAG)] + [("Y", 0)]
    + [("U", n) for n in range(EXPERTS + LAG, UNITS + LAG)] + [("Y", 1)])

MISC_BANKS = (6, 7)
USES = {"A": ["xT"], "B": ["q", "k"], "X": ["eT"], "V": ["v"], "C": ["S"], "D": ["PT"], "E": ["PV"], "F": ["sT"],
        "H": ["es0", "es1"], "R": ["r"], "G": ["s2T"], "L": ["lg"], "T": ["dT"], "Y": ["y"]}


def misc_turns():
    turns, used = {("bias", 0): (0, 1)}, [1, 0]
    at = 1
    for name, i in SCHEDULE:
        for use in USES.get(name, []):
            slot = at % 2
            used[slot] += 1
            turns[use, i] = (slot, used[slot])
            at += 1
    return turns


def hybrid_kernel(nc, x, wq, bq, wk, bk, wv, bv, gamma, Q, E, gate_w, gate_b, w1, w2, w3, d_scratch, out):
    turns = misc_turns()
    x_tok = x.rearrange("b h w c -> (b h w) c").rearrange("(t p) c -> p t c", p=P)
    out_tok = out.rearrange("b h w c -> (b h w) c").rearrange("(t p) c -> p t c", p=P)
    NT = IMAGES * TILES

    ctx = ExitStack()
    with ctx:
        def sb(name, shape, dt=FP32):
            return ctx.enter_context(nc.sbuf_tensor(name, shape, dt))

        def sem(name):
            return ctx.enter_context(nc.semaphore(name))

        ident = sb("ident", [P, P])
        twin = sb("twin", [P, C])
        causal = sb("causal", [P, P])
        one = sb("one", [1, 1])
        lo_rows = sb("lo_rows", [P, 2])
        neg_half = sb("neg_half", [P, TILES])
        xd = sb("xd", [P, NT, 2, C])
        wqk_in = sb("wqk_in", [P, 2, QK])
        b_in = sb("b_in", [1, 2, QK])
        b_row = sb("b_row", [1, 2, 4, 32])
        wv_in = sb("wv_in", [P, C])
        bv_in = sb("bv_in", [P, C])
        gamma_in = sb("gamma_in", [P, 1])
        q_in = sb("q_in", [P, HEADS, C])
        e_in = sb("e_in", [P, PAIRS, 2, C])
        gate_in = sb("gate_in", [P, EXPERTS])
        gate_b_in = sb("gate_b_in", [P, EXPERTS])
        w_in = sb("w_in", [P, 2, EXPERTS * HIDDEN])
        w3_in = sb("w3_in", [P, EXPERTS, C])
        wqk = [sb(f"wqk_{s}", [P, 2, 4, 32], F32R) for s in ("hi", "lo")]
        wvs = [sb(f"wv_{s}", [P, C], F32R) for s in ("hi", "lo")]
        Qs = [sb(f"Q_{s}", [P, HEADS, 2, C], F32R) for s in ("hi", "lo")]
        Es = [sb(f"E_{s}", [P, HEADS * C], F32R) for s in ("hi", "lo")]
        gates = [sb(f"gate_{s}", [P, EXPERTS], F32R) for s in ("hi", "lo")]
        ws = [sb(f"w_{s}", [P, 2, EXPERTS * HIDDEN], F32R) for s in ("hi", "lo")]
        xT = sb("xT", [P, IMAGES * TOKENS], F32R)
        sT = sb("sT", [P, IMAGES * TOKENS], F32R)
        s2T = sb("s2T", [P, IMAGES * TOKENS], F32R)
        b_col = sb("b_col", [P, 4])
        hi_part = sb("hi_part", [P, 2, 2, TOKENS], F32R)
        qk = sb("qk", [P, 2, 2, TOKENS], F32R)
        v = sb("v", [P, IMAGES, TILES, C + 1])
        nmax = sb("nmax", [P, 2, TILES])
        prob = sb("prob", [P, 2, TILES, TOKENS])
        probT = sb("probT", [P, 2, TILES, TOKENS])
        rsum = sb("rsum", [P, 2, 2, TILES])
        x1 = sb("x1", [P, NT, C])
        x2 = sb("x2", [P, NT, C])
        stats = sb("stats", [P, 2, TILES, 6])
        mv = sb("mv", [P, 2, IMAGES, TILES, 2])
        veps = sb("veps", [P, 2, IMAGES, TILES])
        rstd = sb("rstd", [P, 2, IMAGES, TILES])
        sd = sb("sd", [P, 2, 2, TILES, 2, C])
        es = sb("es", [P, 2, TILES, HEADS * C])
        q_parts = [sb(f"qs_{s}", [P, 2, 2, TOKENS], F32R) for s in ("hi", "lo")]
        omega = sb("omega", [P, 2, 2, 3, P])
        rts = sb("rts", [P, 2, TOKENS])
        lg = sb("lg", [P, HTILES, EXPERTS])
        lmax = sb("lmax", [P, HTILES])
        gp = sb("gp", [P, HTILES, EXPERTS])
        gsum = sb("gsum", [P, HTILES])
        grec = sb("grec", [P, HTILES])
        probs = sb("probs", [P, HTILES, EXPERTS])
        top8 = sb("top8", [P, HTILES, 8])
        rest = sb("rest", [P, HTILES, EXPERTS])
        tsum = sb("tsum", [P, HTILES])
        trec = sb("trec", [P, HTILES])
        dsel = sb("dsel", [P, HTILES, EXPERTS])
        disp = sb("disp", [P, HTILES, EXPERTS])
        dispT = sb("dispT", [HTILES * EXPERTS, HALVES, P])
        dbc = sb("dbc", [P, EXPERTS, HALF])
        sil = sb("sil", [P, SIL, HALF])
        uu = sb("uu", [P, UU, HALF])
        hid = sb("hid", [P, HID, HALF])
        yts = sb("yts", [P, HALVES, HALF])
        res = sb("res", [P, NT, C])

        banks = [ctx.enter_context(nc.psum_tensor(f"bank{i}", [P, 512], FP32)) for i in range(8)]
        Q_BANK, DIAG_BANK, OFF_BANK, RT_BANK = (0, 1), (2, 3), 4, 5
        U1_BANK, U2_BANK, Y_BANK = (0, 1), (2, 3), (4, 5)

        ld_x = [sem(f"ld_x{b}") for b in range(IMAGES)]
        ld_wqk, ld_b, ld_v, ld_gamma, ld_q, ld_e = (sem("ld_" + n) for n in ("wqk", "b", "v", "gamma", "q", "e"))
        ld_gate, ld_w, ld_w3 = sem("ld_gate"), sem("ld_w"), sem("ld_w3")
        zeroed, consts = sem("zeroed"), sem("consts")
        b_row_ready, wqk_ready, wv_ready = sem("b_row_ready"), sem("wqk_ready"), sem("wv_ready")
        Q_ready, gate_ready, w_ready = sem("Q_ready"), sem("gate_ready"), sem("w_ready")
        E_hi_done, E_lo_done = sem("E_hi_done"), sem("E_lo_done")
        filled = [sem(f"filled{i}") for i in range(2)]
        emptied = [sem(f"emptied{i}") for i in range(2)]
        xT_hi, qk_hi, sT_hi, s2T_hi = sem("xT_hi"), sem("qk_hi"), sem("sT_hi"), sem("s2T_hi")
        nmax_ready = sem("nmax_ready")
        var_ready = [sem("var1_ready"), sem("var2_ready")]
        rstd_ready = [sem("rstd1_ready"), sem("rstd2_ready")]
        sd_ready = [sem("sd1_ready"), sem("sd2_ready")]
        q_filled, qhi_done, qlo_done = sem("q_filled"), sem("qhi_done"), sem("qlo_done")
        diag_filled, off_filled, diag_done, off_done = (sem(n) for n in ("diag_filled", "off_filled", "diag_done", "off_done"))
        r_done, rts_done = sem("r_done"), sem("rts_done")
        lg_ready, gexp_done, disp_ready = sem("lg_ready"), sem("gexp_done"), sem("disp_ready")
        d_stored = sem("d_stored")
        dbc_ld = [[sem(f"dbc_ld{h}_{c}") for c in range(4)] for h in range(HALVES)]
        u1_filled, u2_filled, sil_done, uu_done, hid_done, down_done = (
            sem(n) for n in ("u1_filled", "u2_filled", "sil_done", "uu_done", "hid_done", "down_done"))
        yts_done, stored = sem("yts_done"), sem("stored")
        dve_step, pool_step = sem("dve_step"), sem("pool_step")

        def bank_of(use, i):
            return banks[MISC_BANKS[turns[use, i][0]]]

        def wait_free(eng, use, i):
            slot, nth = turns[use, i]
            if nth > 1:
                eng.wait_ge(emptied[slot], nth - 1)

        def wait_filled(eng, use, i):
            slot, nth = turns[use, i]
            eng.wait_ge(filled[slot], nth)

        def wait_emptied(eng, use, i):
            slot, nth = turns[use, i]
            eng.wait_ge(emptied[slot], nth)

        def is_filled(use, i):
            return filled[turns[use, i][0]]

        def is_emptied(use, i):
            return emptied[turns[use, i][0]]

        def img(b):
            return slice(b * TOKENS, (b + 1) * TOKENS)

        def tile(t):
            return slice(t * P, (t + 1) * P)

        block = ctx.enter_context(nc.Block())

        @block.sync
        def _(sp):
            def load_x(b):
                for half in range(2):
                    sp.dma_start(xd[:, TILES * b:TILES * (b + 1), half, :],
                                 x_tok[:, TILES * b:TILES * (b + 1), :]).then_inc(ld_x[b], 16)

            def load_twice(dst, src, s):
                for half in range(2):
                    sp.dma_start(dst[C * half:C * (half + 1)], src).then_inc(s, 16)

            load_x(0)
            load_twice(wqk_in[:, 0, :], wq, ld_wqk)
            load_twice(wqk_in[:, 1, :], wk, ld_wqk)
            load_x(1)
            load_twice(wv_in[:], wv, ld_v)
            load_twice(q_in[:], Q.rearrange("h i j -> i h j"), ld_q)
            load_x(2)
            load_x(3)
            load_twice(gate_in[:], gate_w, ld_gate)
            for m, w in enumerate((w1, w2)):
                for half in range(2):
                    sp.dma_start(w_in[C * half:C * (half + 1), m, :].rearrange("c (e h) -> c e h", e=EXPERTS),
                                 w.rearrange("e c h -> c e h")).then_inc(ld_w, 16)
            sp.dma_start(w3_in[:], w3.rearrange("e h c -> h e c")).then_inc(ld_w3, 16)
            for name, i in SCHEDULE:
                if name == "T":
                    wait_emptied(sp, "dT", i)
                    sp.dma_start(d_scratch[i].rearrange("e (t p) -> t e p", p=P), dispT[:, i, :]).then_inc(d_stored, 16)
                    sp.wait_ge(d_stored, 16 * (i + 1))
                    for c in range(4):
                        if i == 1:
                            sp.wait_ge(hid_done, 4 * (c + 1))
                        src = d_scratch[i, 4 * c:4 * (c + 1), :].rearrange("e t -> (e t)").unsqueeze(0)
                        sp.dma_start(dbc[:, 4 * c:4 * (c + 1), :].rearrange("p e t -> p (e t)"),
                                     src.to_broadcast([P, 4 * HALF])).then_inc(dbc_ld[i][c], 16)
                if name == "Y":
                    wait_emptied(sp, "y", i)
                    sp.dma_start(out_tok[:, HTILES * i:HTILES * (i + 1), :],
                                 res[:, HTILES * i:HTILES * (i + 1), :]).then_inc(stored, 16)
            sp.wait_ge(stored, 16 * HALVES)

        @block.gpsimd
        def _(pool):
            def wait_step(ins, count=[0]):
                count[0] += 1
                ins.then_inc(pool_step, 1)
                pool.wait_ge(pool_step, count[0])

            pool.memset(ident[:], 0.0).then_inc(zeroed, 1)
            pool.memset(b_row[:], 0.0).then_inc(zeroed, 1)
            for part in wqk:
                pool.memset(part[:].bitcast(FP32), 0.0).then_inc(zeroed, 1)
            pool.wait_ge(zeroed, 4)
            pool.affine_select(out=ident[:], in_=ident[:], compare_op=ALU.not_equal, fill=1.0, base=0,
                               pattern=[[-1, P]], channel_multiplier=1).then_inc(consts, 1)
            pool.memset(one[:], 1.0).then_inc(consts, 1)
            pool.memset(v[:, :, :, C:C + 1], 1.0).then_inc(consts, 1)
            pool.memset(neg_half[:], -0.5).then_inc(consts, 1)
            pool.memset(causal[:], 1.0).then_inc(zeroed, 1)
            pool.memset(twin[:], 0.0).then_inc(zeroed, 1)
            pool.wait_ge(zeroed, 6)
            pool.affine_select(out=causal[:], in_=causal[:], compare_op=ALU.is_ge, fill=0.0, base=0,
                               pattern=[[1, P]], channel_multiplier=-1).then_inc(consts, 1)
            wait_step(pool.affine_select(out=twin[:], in_=twin[:], compare_op=ALU.not_equal, fill=1.0, base=0,
                                         pattern=[[-1, C]], channel_multiplier=1))
            pool.affine_select(out=twin[:], in_=twin[:], compare_op=ALU.not_equal, fill=1.0, base=-C,
                               pattern=[[-1, C]], channel_multiplier=1).then_inc(consts, 1)
            pool.wait_ge(ld_q, 32)
            q_twice = q_in[:].unsqueeze(2).to_broadcast([P, HEADS, 2, C])
            for h in range(0, HEADS, 4):
                wait_step(nc.gpsimd.tensor_copy(Qs[0][:, h:h + 4], q_twice[:, h:h + 4]))
                nc.gpsimd.tensor_tensor(Qs[1][:, h:h + 4], q_twice[:, h:h + 4], Qs[0][:, h:h + 4].bitcast(FP32),
                                        ALU.subtract).then_inc(Q_ready, 1)

            def reciprocal_deviation(norm, b, eps):
                pool.wait_ge(var_ready[norm], b + 1)
                wait_step(nc.gpsimd.tensor_scalar(veps[:, norm, b, :], mv[:, norm, b, :, 1], eps, None, ALU.add))
                nc.gpsimd.tensor_tensor(rstd[:, norm, b, :], veps[:, norm, b, :], neg_half[:],
                                        ALU.pow).then_inc(rstd_ready[norm], 1)

            for name, i in SCHEDULE:
                if name == "E":
                    reciprocal_deviation(0, i, 1e-5)
                if name == "R":
                    reciprocal_deviation(1, i, 1e-5)
                if name == "W":
                    if i == 0:
                        pool.wait_ge(ld_gate, 48)
                        wait_step(nc.gpsimd.tensor_copy(gates[0][:], gate_in[:]))
                        nc.gpsimd.tensor_tensor(gates[1][:], gate_in[:], gates[0][:].bitcast(FP32),
                                                ALU.subtract).then_inc(gate_ready, 1)
                        pool.wait_ge(ld_w, 64)
                    cols = slice(2 * i * HIDDEN, 2 * (i + 1) * HIDDEN)
                    wait_step(nc.gpsimd.tensor_copy(ws[0][:, :, cols], w_in[:, :, cols]))
                    nc.gpsimd.tensor_tensor(ws[1][:, :, cols], w_in[:, :, cols], ws[0][:, :, cols].bitcast(FP32),
                                            ALU.subtract).then_inc(w_ready, 1)
                if name == "U" and i < UNITS:
                    half, e = divmod(i, EXPERTS)
                    pool.wait_ge(uu_done, i + 1)
                    if e % 4 == 0:
                        pool.wait_ge(dbc_ld[half][e // 4], 16)
                    if i >= HID:
                        pool.wait_ge(down_done, (i - HID) // 2 + 1)
                    nc.gpsimd.tensor_tensor(hid[:, i % HID], uu[:, i % UU], dbc[:, e, :],
                                            ALU.mult).then_inc(hid_done, 1)

        @block.scalar
        def _(act):
            act.dma_start(b_in[0:1, 0, :], bq.unsqueeze(0)).then_inc(ld_b, 16)
            act.dma_start(b_in[0:1, 1, :], bk.unsqueeze(0)).then_inc(ld_b, 16)
            for twice in range(2):
                act.dma_start(e_in[:, :, twice, :],
                              E.rearrange("(m g) i k -> (g i) m k", g=2)).then_inc(ld_e, 16)
            act.dma_start(bv_in[:], bv.unsqueeze(0).to_broadcast([P, C])).then_inc(ld_v, 16)
            act.dma_start(gamma_in[:], gamma.unsqueeze(0).to_broadcast([P, 1])).then_inc(ld_gamma, 16)
            act.dma_start(gate_b_in[:], gate_b.unsqueeze(0).to_broadcast([P, EXPERTS])).then_inc(ld_gate, 16)

            def query_hi(g):
                act.wait_ge(q_filled, g + 1)
                if g >= 2:
                    act.wait_ge(off_filled, g - 1)
                nc.scalar.activation(q_parts[0][:, g % 2].rearrange("p h t -> p (h t)"), banks[Q_BANK[g % 2]][:],
                                     ACT.Copy).then_inc(qhi_done, 1)

            for name, i in SCHEDULE:
                if name == "A":
                    wait_filled(act, "xT", i)
                    nc.scalar.activation(xT[:, img(i)], bank_of("xT", i)[:, 0:TOKENS], ACT.Copy).then_inc(xT_hi, 1)
                if name == "X":
                    wait_filled(act, "eT", 0)
                    nc.scalar.activation(Es[0][:], bank_of("eT", 0)[:], ACT.Copy).then_inc(E_hi_done, 1)
                if name == "B":
                    for m, use in enumerate("qk"):
                        if i == 0 and m == 0:
                            wait_emptied(act, "bias", 0)
                        wait_filled(act, use, i)
                        if i >= 2:
                            wait_emptied(act, use, i - 2)
                        nc.scalar.activation(hi_part[:, i % 2, m, :], bank_of(use, i)[:, 0:TOKENS], ACT.Identity,
                                             bias=b_col[:, 2 + m:3 + m], scale=lo_rows[:, m:m + 1]).then_inc(qk_hi, 1)
                if name == "C":
                    act.wait_ge(nmax_ready, i + 1)
                    for k in range(TILES):
                        last = nc.scalar.activation(prob[:, i % 2, k, :], bank_of("S", i)[:, k * TOKENS:(k + 1) * TOKENS],
                                                    ACT.Exp, bias=nmax[:, i % 2, k:k + 1])
                    last.then_inc(is_emptied("S", i), 1)
                if name == "D":
                    wait_filled(act, "PT", i)
                    if i >= 2:
                        wait_filled(act, "PV", i - 2)
                    nc.scalar.activation(probT[:, i % 2].rearrange("p j n -> p (j n)"), bank_of("PT", i)[:],
                                         ACT.Copy).then_inc(is_emptied("PT", i), 1)
                if name == "F":
                    wait_filled(act, "sT", i)
                    nc.scalar.activation(sT[:, img(i)], bank_of("sT", i)[:, 0:TOKENS], ACT.Copy).then_inc(sT_hi, 1)
                if name == "H":
                    wait_filled(act, "es0", i)
                    if i >= 2:
                        act.wait_ge(r_done, PAIRS * (i - 1))
                    nc.scalar.activation(es[:, i % 2, 0, :], bank_of("es0", i)[:],
                                         ACT.Copy).then_inc(is_emptied("es0", i), 1)
                if name == "P":
                    if i == 0:
                        query_hi(0)
                    if i + 1 < IMAGES * PAIRS:
                        query_hi(i + 1)
                    if i < IMAGES * PAIRS:
                        act.wait_ge(off_filled, i + 1)
                        if i >= 2:
                            act.wait_ge(r_done, i - 1)
                        nc.scalar.activation(omega[:, i % 2, :, 1, :],
                                             banks[OFF_BANK][:, 0:2 * P].rearrange("p (h t) -> p h t", h=2),
                                             ACT.Copy).then_inc(off_done, 1)
                if name == "N":
                    act.wait_ge(r_done, PAIRS * (i + 1))
                    if i >= 2:
                        wait_filled(act, "r", i - 2)
                    nc.scalar.activation(rts[:, i % 2, :], banks[RT_BANK][:, 0:TOKENS], ACT.Copy).then_inc(rts_done, 1)
                if name == "G":
                    wait_filled(act, "s2T", i)
                    nc.scalar.activation(s2T[:, img(i)], bank_of("s2T", i)[:, 0:TOKENS], ACT.Copy).then_inc(s2T_hi, 1)
                if name == "L":
                    act.wait_ge(lg_ready, i + 1)
                    nc.scalar.activation(gp[:], lg[:], ACT.Exp).then_inc(gexp_done, 1)
                if name == "T":
                    wait_filled(act, "dT", i)
                    nc.scalar.activation(dispT[:, i, :], bank_of("dT", i)[0:HTILES * EXPERTS, 0:P],
                                         ACT.Copy).then_inc(is_emptied("dT", i), 1)
                if name == "U" and i < UNITS:
                    act.wait_ge(u1_filled, i + 1)
                    if i >= SIL:
                        act.wait_ge(uu_done, i - SIL + 1)
                    nc.scalar.activation(sil[:, i % SIL], banks[U1_BANK[i % 2]][:], ACT.Silu).then_inc(sil_done, 1)
                if name == "Y":
                    act.wait_ge(down_done, EXPERTS // 2 * (i + 1))
                    nc.scalar.activation(yts[:, i, :], banks[Y_BANK[i]][:], ACT.Copy).then_inc(yts_done, 1)

        @block.vector
        def _(dve):
            def wait_step(ins, count=[0]):
                count[0] += 1
                ins.then_inc(dve_step, 1)
                dve.wait_ge(dve_step, count[0])

            def lo_half(stack, hi_sem, use, b):
                dve.wait_ge(hi_sem, b + 1)
                nc.vector.tensor_tensor(stack[C:P, img(b)], bank_of(use, b)[C:P, 0:TOKENS],
                                        stack[C:P, img(b)].bitcast(FP32), ALU.subtract).then_inc(is_emptied(use, b), 1)

            def statistics(norm, b, src):
                for k in range(TILES):
                    last = nc.vector.bn_stats(stats[:, norm, k, :], src[:, TILES * b + k, :])
                wait_step(last)
                for k in range(TILES):
                    last = nc.vector.bn_aggr(mv[:, norm, b, k, :], stats[:, norm, k, :])
                last.then_inc(var_ready[norm], 1)

            def normalise(norm, b, src):
                dve.wait_ge(rstd_ready[norm], b + 1)
                for k in range(TILES):
                    last = nc.vector.tensor_scalar(
                        sd[:, norm, b % 2, k], src[:, TILES * b + k, :].unsqueeze(1).to_broadcast([P, 2, C]),
                        mv[:, norm, b, k, 0:1], rstd[:, norm, b, k:k + 1], ALU.subtract, ALU.mult)
                last.then_inc(sd_ready[norm], 1)

            def query_lo(g):
                dve.wait_ge(qhi_done, g + 1)
                nc.vector.tensor_tensor(q_parts[1][:, g % 2].rearrange("p h t -> p (h t)"), banks[Q_BANK[g % 2]][:],
                                        q_parts[0][:, g % 2].rearrange("p h t -> p (h t)").bitcast(FP32),
                                        ALU.subtract).then_inc(qlo_done, 1)

            wait_step(nc.vector.memset(lo_rows[:], 0.0))
            for rows, m in ((slice(32, 64), 0), (slice(96, 128), 0), (slice(64, 128), 1)):
                wait_step(nc.vector.memset(lo_rows[rows, m:m + 1], 1.0))
            dve.wait_ge(zeroed, 4)
            dve.wait_ge(ld_b, 32)
            nc.vector.tensor_copy(b_row[0:1, :, :, 0:QK],
                                  b_in[0:1].unsqueeze(2).to_broadcast([1, 2, 4, QK])).then_inc(b_row_ready, 1)
            dve.wait_ge(ld_wqk, 64)
            for m in range(2):
                four = wqk_in[:, m, :].unsqueeze(1).to_broadcast([P, 4, QK])
                wait_step(nc.vector.tensor_copy(wqk[0][:, m, :, 0:QK], four))
                last = nc.vector.tensor_tensor(wqk[1][:, m, :, 0:QK], four, wqk[0][:, m, :, 0:QK].bitcast(FP32),
                                               ALU.subtract)
            last.then_inc(wqk_ready, 1)
            wait_filled(dve, "bias", 0)
            wait_step(nc.vector.tensor_copy(b_col[:, 0:2], bank_of("bias", 0)[:, 0:2]))
            nc.vector.tensor_tensor(b_col[:, 2:4], b_col[:, 0:2], lo_rows[:], ALU.mult).then_inc(is_emptied("bias", 0), 1)

            for name, i in SCHEDULE:
                if name == "A":
                    lo_half(xT, xT_hi, "xT", i)
                    if i == 0:
                        dve.wait_ge(ld_v, 48)
                        wait_step(nc.vector.tensor_copy(wvs[0][:], wv_in[:]))
                        nc.vector.tensor_tensor(wvs[1][:], wv_in[:], wvs[0][:].bitcast(FP32),
                                                ALU.subtract).then_inc(wv_ready, 1)
                if name == "X":
                    dve.wait_ge(E_hi_done, 1)
                    nc.vector.tensor_tensor(Es[1][:], bank_of("eT", 0)[:], Es[0][:].bitcast(FP32),
                                            ALU.subtract).then_inc(is_emptied("eT", 0), 1)
                if name == "B":
                    for m, use in enumerate("qk"):
                        if i == 0 and m == 0:
                            wait_emptied(dve, "bias", 0)
                        dve.wait_ge(qk_hi, 2 * i + m + 1)
                        nc.vector.scalar_tensor_tensor(out=qk[:, i % 2, m, :], in0=bank_of(use, i)[:, 0:TOKENS],
                                                       scalar=b_col[:, m:m + 1], in1=hi_part[:, i % 2, m, :].bitcast(FP32),
                                                       op0=ALU.add, op1=ALU.subtract).then_inc(is_emptied(use, i), 1)
                if name == "V":
                    wait_filled(dve, "v", i)
                    if i == 0:
                        dve.wait_ge(consts, 3)
                    nc.vector.tensor_tensor(v[:, i, :, 0:C],
                                            bank_of("v", i)[:, 0:TILES * C].rearrange("p (k c) -> p k c", k=TILES),
                                            bv_in[:].unsqueeze(1).to_broadcast([P, TILES, C]),
                                            ALU.add).then_inc(is_emptied("v", i), 1)
                if name == "C":
                    wait_filled(dve, "S", i)
                    nc.vector.tensor_reduce(nmax[:, i % 2, :],
                                            bank_of("S", i)[:].rearrange("p (k m) -> p k m", k=TILES), AX.X, ALU.max,
                                            negate=True).then_inc(nmax_ready, 1)
                if name == "E":
                    wait_filled(dve, "PV", i)
                    if i == 0:
                        dve.wait_ge(ld_gamma, 16)
                    pv = bank_of("PV", i)[:, 0:TILES * (C + 1)].rearrange("p (k c) -> p k c", k=TILES)
                    wait_step(nc.vector.reciprocal(rsum[:, i % 2, 0, :], pv[:, :, C]))
                    wait_step(nc.vector.tensor_scalar(rsum[:, i % 2, 1, :], rsum[:, i % 2, 0, :], gamma_in[:, 0:1], None,
                                                      ALU.mult))
                    for k in range(TILES):
                        last = nc.vector.scalar_tensor_tensor(
                            out=x1[:, TILES * i + k, :], in0=pv[:, k, 0:C], scalar=rsum[:, i % 2, 1, k:k + 1],
                            in1=xd[:, TILES * i + k, 0, :], op0=ALU.mult, op1=ALU.add)
                    last.then_inc(is_emptied("PV", i), 1)
                    wait_emptied(dve, "PV", i)
                    statistics(0, i, x1)
                if name == "F":
                    normalise(0, i, x1)
                    lo_half(sT, sT_hi, "sT", i)
                if name == "H":
                    wait_filled(dve, "es1", i)
                    if i >= 2:
                        dve.wait_ge(r_done, PAIRS * (i - 1))
                    nc.vector.tensor_copy(es[:, i % 2, 1, :], bank_of("es1", i)[:]).then_inc(is_emptied("es1", i), 1)
                if name == "P":
                    if i == 0:
                        dve.wait_ge(consts, 5)
                        query_lo(0)
                    if i + 1 < IMAGES * PAIRS:
                        query_lo(i + 1)
                    if i < IMAGES * PAIRS:
                        dve.wait_ge(diag_filled, i + 1)
                        if i >= 2:
                            dve.wait_ge(r_done, i - 1)
                        for d in range(2):
                            last = nc.vector.tensor_tensor(
                                omega[:, i % 2, :, 2 * d, :],
                                banks[DIAG_BANK[i % 2]][:, 2 * P * d:2 * P * (d + 1)].rearrange("p (h t) -> p h t", h=2),
                                causal[:].unsqueeze(1).to_broadcast([P, 2, P]), ALU.mult)
                        last.then_inc(diag_done, 1)
                if name == "R":
                    wait_filled(dve, "r", i)
                    nc.vector.tensor_tensor(x2[:, TILES * i:TILES * (i + 1), :], x1[:, TILES * i:TILES * (i + 1), :],
                                            bank_of("r", i)[:, 0:TILES * C].rearrange("p (k c) -> p k c", k=TILES),
                                            ALU.add).then_inc(is_emptied("r", i), 1)
                    wait_emptied(dve, "r", i)
                    statistics(1, i, x2)
                if name == "G":
                    normalise(1, i, x2)
                    lo_half(s2T, s2T_hi, "s2T", i)
                if name == "L":
                    wait_filled(dve, "lg", i)
                    if i == 0:
                        dve.wait_ge(ld_gate, 48)
                    lg_psum = bank_of("lg", i)[:, 0:HTILES * EXPERTS].rearrange("p (t e) -> p t e", t=HTILES)
                    nc.vector.tensor_tensor(lg[:], lg_psum, gate_b_in[:].unsqueeze(1).to_broadcast([P, HTILES, EXPERTS]),
                                            ALU.add).then_inc(is_emptied("lg", i), 1)
                    wait_emptied(dve, "lg", i)
                    wait_step(nc.vector.tensor_reduce(lmax[:], lg[:], AX.X, ALU.max))
                    nc.vector.tensor_tensor(lg[:], lg[:], lmax[:].unsqueeze(2).to_broadcast([P, HTILES, EXPERTS]),
                                            ALU.subtract).then_inc(lg_ready, 1)
                if name == "M":
                    spread = [P, HTILES, EXPERTS]
                    dve.wait_ge(gexp_done, i + 1)
                    wait_step(nc.vector.tensor_reduce(gsum[:], gp[:], AX.X, ALU.add))
                    wait_step(nc.vector.reciprocal(grec[:], gsum[:]))
                    wait_step(nc.vector.tensor_tensor(probs[:], gp[:], grec[:].unsqueeze(2).to_broadcast(spread), ALU.mult))
                    for t in range(HTILES):
                        last = nc.vector.max(top8[:, t, :], probs[:, t, :])
                    wait_step(last)
                    wait_step(nc.vector.tensor_tensor(tsum[:], top8[:, :, 0], top8[:, :, 1], ALU.add))
                    nc.vector.reciprocal(trec[:], tsum[:])
                    wait_step(nc.vector.memset(top8[:, :, 2:8], -1.0))
                    for t in range(HTILES):
                        last = nc.vector.match_replace(out=rest[:, t, :], in_to_replace=top8[:, t, :],
                                                       in_values=probs[:, t, :], imm_value=0.0)
                    wait_step(last)
                    wait_step(nc.vector.tensor_tensor(dsel[:], probs[:], rest[:], ALU.subtract))
                    nc.vector.tensor_tensor(disp[:], dsel[:], trec[:].unsqueeze(2).to_broadcast(spread),
                                            ALU.mult).then_inc(disp_ready, 1)
                if name == "U" and i < UNITS:
                    dve.wait_ge(u2_filled, i + 1)
                    dve.wait_ge(sil_done, i + 1)
                    if i >= UU:
                        dve.wait_ge(hid_done, i - UU + 1)
                    nc.vector.tensor_tensor(uu[:, i % UU], banks[U2_BANK[i % 2]][:], sil[:, i % SIL],
                                            ALU.mult).then_inc(uu_done, 1)
                if name == "Y":
                    wait_filled(dve, "y", i)
                    nc.vector.tensor_tensor(res[:, HTILES * i:HTILES * (i + 1), :], x2[:, HTILES * i:HTILES * (i + 1), :],
                                            bank_of("y", i)[:, 0:HTILES * C].rearrange("p (t c) -> p t c", t=HTILES),
                                            ALU.add).then_inc(is_emptied("y", i), 1)

        @block.tensor
        def _(pe):
            def two_pass(dst, weights, moving):
                nc.tensor.matmul(dst, weights[0], moving[0], start=True, stop=False)
                return nc.tensor.matmul(dst, weights[1], moving[1], start=False, stop=True)

            def transpose_tiles(use, b, tiles):
                for k, src in enumerate(tiles):
                    last = nc.tensor.transpose(bank_of(use, b)[:, tile(k)], src, ident[:])
                last.then_inc(is_filled(use, b), 1)

            def queries(g):
                b, pair = divmod(g, PAIRS)
                if pair == 0:
                    wait_emptied(pe, "sT", b)
                if g < 2:
                    pe.wait_ge(Q_ready, 1)
                elif g == 2:
                    pe.wait_ge(Q_ready, 2)
                if g >= 2:
                    pe.wait_ge(qlo_done, g - 1)
                for hh in range(2):
                    h = 2 * pair + hh
                    last = two_pass(banks[Q_BANK[g % 2]][:, hh * TOKENS:(hh + 1) * TOKENS],
                                    [part[:, h].rearrange("p d j -> p (d j)") for part in Qs], [sT[:, img(b)]] * 2)
                last.then_inc(q_filled, 1)

            def scores(g):
                b = g // PAIRS
                pe.wait_ge(qlo_done, g + 1)
                u = [sT[:, tile(TILES * b + k)] for k in range(TILES)]
                at = [[part[:, g % 2, :, tile(k)] for part in q_parts] for k in range(TILES)]
                if g >= 2:
                    pe.wait_ge(diag_done, g - 1)
                two_pass(banks[DIAG_BANK[g % 2]][:, 0:2 * P], [u[0]] * 2, at[0])
                two_pass(banks[DIAG_BANK[g % 2]][:, 2 * P:4 * P], [u[1]] * 2, at[1]).then_inc(diag_filled, 1)
                if g >= 1:
                    pe.wait_ge(off_done, g)
                two_pass(banks[OFF_BANK][:, 0:2 * P], [u[0]] * 2, at[1]).then_inc(off_filled, 1)

            def head_sums(g):
                b, pair = divmod(g, PAIRS)
                pe.wait_ge(diag_done, g + 1)
                pe.wait_ge(off_done, g + 1)
                if pair == 0:
                    wait_emptied(pe, "es0", b)
                    wait_emptied(pe, "es1", b)
                    if b >= 1:
                        pe.wait_ge(rts_done, b)
                for u in range(2):
                    for hh in range(2):
                        h = 2 * pair + hh
                        blocks = omega[:, g % 2, hh, 2 * u:2 + u, :].rearrange("p k t -> p (k t)")
                        last = nc.tensor.matmul(banks[RT_BANK][C * hh:C * (hh + 1), P * u:TOKENS],
                                                es[:, b % 2, u, C * h:C * (h + 1)], blocks,
                                                start=(pair == 0 and u == 0), stop=(pair == PAIRS - 1 and u == 1))
                last.then_inc(r_done, 1)

            pe.wait_ge(consts, 2)
            pe.wait_ge(b_row_ready, 1)
            for m in range(2):
                last = nc.tensor.matmul(bank_of("bias", 0)[:, m:m + 1], b_row[0:1, m].rearrange("o g n -> o (g n)"),
                                        one[0:1, 0:1], start=True, stop=True)
            last.then_inc(is_filled("bias", 0), 1)

            for name, i in SCHEDULE:
                if name == "A":
                    pe.wait_ge(ld_x[i], 32)
                    wait_free(pe, "xT", i)
                    transpose_tiles("xT", i, [xd[:, TILES * i + k].rearrange("p d c -> p (d c)") for k in range(TILES)])
                if name == "X":
                    pe.wait_ge(ld_e, 32)
                    wait_free(pe, "eT", i)
                    transpose_tiles("eT", i, [e_in[:, m].rearrange("p d k -> p (d k)") for m in range(PAIRS)])
                if name == "B":
                    if i == 0:
                        pe.wait_ge(wqk_ready, 1)
                    wait_emptied(pe, "xT", i)
                    for m, use in enumerate("qk"):
                        wait_free(pe, use, i)
                        two_pass(bank_of(use, i)[:, 0:TOKENS], [part[:, m].rearrange("p g n -> p (g n)") for part in wqk],
                                 [xT[:, img(i)]] * 2).then_inc(is_filled(use, i), 1)
                if name == "V":
                    if i == 0:
                        pe.wait_ge(wv_ready, 1)
                    wait_free(pe, "v", i)
                    for k in range(TILES):
                        last = two_pass(bank_of("v", i)[:, C * k:C * (k + 1)], [xT[:, tile(TILES * i + k)]] * 2,
                                        [part[:] for part in wvs])
                    last.then_inc(is_filled("v", i), 1)
                if name == "C":
                    wait_emptied(pe, "q", i)
                    wait_emptied(pe, "k", i)
                    wait_free(pe, "S", i)
                    for k in range(TILES):
                        last = nc.tensor.matmul(bank_of("S", i)[:, k * TOKENS:(k + 1) * TOKENS], qk[:, i % 2, 0, tile(k)],
                                                qk[:, i % 2, 1, :], start=True, stop=True)
                    last.then_inc(is_filled("S", i), 1)
                if name == "D":
                    wait_emptied(pe, "S", i)
                    wait_free(pe, "PT", i)
                    transpose_tiles("PT", i, [prob[:, i % 2, k, tile(j)] for j in range(TILES) for k in range(TILES)])
                if name == "E":
                    wait_emptied(pe, "PT", i)
                    wait_emptied(pe, "v", i)
                    wait_free(pe, "PV", i)
                    for k in range(TILES):
                        for j in range(TILES):
                            last = nc.tensor.matmul(bank_of("PV", i)[:, (C + 1) * k:(C + 1) * (k + 1)],
                                                    probT[:, i % 2, j, tile(k)], v[:, i, j, :],
                                                    start=(j == 0), stop=(j == TILES - 1))
                    last.then_inc(is_filled("PV", i), 1)
                if name == "F":
                    pe.wait_ge(sd_ready[0], i + 1)
                    wait_free(pe, "sT", i)
                    transpose_tiles("sT", i, [sd[:, 0, i % 2, k].rearrange("p d c -> p (d c)") for k in range(TILES)])
                if name == "H":
                    if i == 0:
                        wait_emptied(pe, "eT", 0)
                    wait_emptied(pe, "sT", i)
                    for u in range(TILES):
                        use = f"es{u}"
                        wait_free(pe, use, i)
                        two_pass(bank_of(use, i)[:], [sT[:, tile(TILES * i + u)]] * 2,
                                 [part[:] for part in Es]).then_inc(is_filled(use, i), 1)
                if name == "P":
                    if i == 0:
                        queries(0)
                    if i + 1 < IMAGES * PAIRS:
                        queries(i + 1)
                    if i < IMAGES * PAIRS:
                        scores(i)
                    if i == 1:
                        pe.wait_ge(consts, 6)
                    if i >= 1:
                        head_sums(i - 1)
                if name == "R":
                    pe.wait_ge(rts_done, i + 1)
                    wait_free(pe, "r", i)
                    for k in range(TILES):
                        last = nc.tensor.matmul(bank_of("r", i)[:, C * k:C * (k + 1)], rts[:, i % 2, tile(k)], twin[:],
                                                start=True, stop=True)
                    last.then_inc(is_filled("r", i), 1)
                if name == "G":
                    pe.wait_ge(sd_ready[1], i + 1)
                    wait_free(pe, "s2T", i)
                    transpose_tiles("s2T", i, [sd[:, 1, i % 2, k].rearrange("p d c -> p (d c)") for k in range(TILES)])
                if name == "L":
                    if i == 0:
                        pe.wait_ge(gate_ready, 1)
                    wait_emptied(pe, "s2T", 2 * i)
                    wait_emptied(pe, "s2T", 2 * i + 1)
                    wait_free(pe, "lg", i)
                    for t in range(HTILES):
                        last = two_pass(bank_of("lg", i)[:, EXPERTS * t:EXPERTS * (t + 1)],
                                        [s2T[:, tile(HTILES * i + t)]] * 2, [part[:] for part in gates])
                    last.then_inc(is_filled("lg", i), 1)
                if name == "T":
                    pe.wait_ge(disp_ready, i + 1)
                    wait_free(pe, "dT", i)
                    nc.tensor.transpose(bank_of("dT", i)[0:HTILES * EXPERTS, 0:P], disp[:].rearrange("p t e -> p (t e)"),
                                        ident[:]).then_inc(is_filled("dT", i), 1)
                if name == "U":
                    if i < UNITS:
                        half, e = divmod(i, EXPERTS)
                        if e == 0:
                            wait_emptied(pe, "s2T", 2 * half)
                            wait_emptied(pe, "s2T", 2 * half + 1)
                        if i < EXPERTS and e % 2 == 0:
                            pe.wait_ge(w_ready, e // 2 + 1)
                        if i < 2:
                            pe.wait_ge(qlo_done, IMAGES * PAIRS - 1 + i)
                            pe.wait_ge(diag_done, IMAGES * PAIRS - 1 + i)
                        else:
                            pe.wait_ge(uu_done, i - 1)
                        moving = s2T[:, half * HALF:(half + 1) * HALF]
                        for m, (bank, full) in enumerate(((U1_BANK, u1_filled), (U2_BANK, u2_filled))):
                            two_pass(banks[bank[i % 2]][:], [part[:, m, HIDDEN * e:HIDDEN * (e + 1)] for part in ws],
                                     [moving] * 2).then_inc(full, 1)
                    if i >= LAG and i % 2 == 0:
                        for n in (i - LAG, i - LAG + 1):
                            half, e = divmod(n, EXPERTS)
                            if e == 0:
                                if half == 0:
                                    pe.wait_ge(ld_w3, 16)
                                    pe.wait_ge(off_done, IMAGES * PAIRS)
                                else:
                                    pe.wait_ge(rts_done, IMAGES)
                            pe.wait_ge(hid_done, n + 1)
                            last = nc.tensor.matmul(banks[Y_BANK[half]][C * (n % 2):C * (n % 2 + 1), :], w3_in[:, e, :],
                                                    hid[:, n % HID], start=(e < 2), stop=(e >= EXPERTS - 2))
                        last.then_inc(down_done, 1)
                if name == "Y":
                    pe.wait_ge(yts_done, i + 1)
                    wait_free(pe, "y", i)
                    for t in range(HTILES):
                        last = nc.tensor.matmul(bank_of("y", i)[:, C * t:C * (t + 1)], yts[:, i, tile(t)], twin[:],
                                                start=True, stop=True)
                    last.then_inc(is_filled("y", i), 1)


_INS = ["x", "L0_conv_wq", "L0_conv_bq", "L0_conv_wk", "L0_conv_bk", "L0_conv_wv", "L0_conv_bv", "L0_conv_gamma",
        "L1_attn_Q", "L1_attn_E", "L1_ffn_gate_w", "L1_ffn_gate_b", "L1_ffn_w1", "L1_ffn_w2", "L1_ffn_w3"]
_OUT = ((4, 16, 16, 64), "float32")


def kernel(**inputs):
    import numpy as _np
    import concourse.bacc as _bacc
    from concourse import mybir as _mybir
    from concourse.bass_utils import run_bass_kernel_spmd as _run

    nc = _bacc.Bacc("TRN2", target_bir_lowering=False, num_devices=1)
    arrays, args = {}, []
    for name in _INS:
        a = _np.ascontiguousarray(inputs[name])
        if a.ndim == 0:
            a = a.reshape(1)
        arrays[f"in_{name}"] = a
        args.append(nc.dram_tensor(f"in_{name}", a.shape, _mybir.dt.from_np(a.dtype), kind="ExternalInput").ap())
    scratch = nc.dram_tensor("dispatch_scratch", (HALVES, EXPERTS, HALF), _mybir.dt.float32).ap()
    shape, dtype = _OUT
    out = nc.dram_tensor("out", shape, _mybir.dt.from_np(_np.dtype(dtype)), kind="ExternalOutput").ap()
    hybrid_kernel(nc, *args, scratch, out)
    result = _run(nc, [arrays], core_ids=[0])
    return result.results[0]["out"]
```

```python
import concourse.bass as bass
from concourse import mybir
from contextlib import ExitStack

FP32 = mybir.dt.float32
F32R = mybir.dt.float32r
ALU = mybir.AluOpType
ACT = mybir.ActivationFunctionType
AX = mybir.AxisListType

P = 128
IMAGES = 4
TOKENS = 256
TILES = TOKENS // P
C = 64
EPS = 1e-5
QK = 8
HEADS = 8
PAIRS = HEADS // 2
EXPERTS = 16
HIDDEN = 128
HALVES = 2
HALF = IMAGES * TOKENS // HALVES
HTILES = HALF // P
UNITS = HALVES * EXPERTS
OM, SIL, UU, HID = 3, 3, 3, 6

SCHEDULE = (
    [("transpose x", 0), ("stack x", 0), ("bias", 0), ("project qk", 0), ("copy qk", 0), ("transpose x", 1),
     ("score", 0), ("stack x", 1), ("project v", 0), ("exp", 0), ("transpose x", 2), ("project qk", 1),
     ("copy qk", 1), ("transpose prob", 0), ("copy v", 0), ("transpose x", 3), ("stack x", 2), ("score", 1),
     ("copy prob", 0), ("attend", 0), ("stack x", 3), ("project v", 1), ("transpose e", 0), ("project qk", 2),
     ("exp", 1), ("residual 1", 0), ("split e", 0), ("split q", 0), ("transpose prob", 1), ("project v", 2),
     ("project v", 3), ("copy v", 1), ("normalise 1", 0), ("transpose s", 0), ("copy v", 2), ("copy prob", 1),
     ("copy v", 3), ("stack s", 0), ("attend", 1), ("split w", 0), ("residual 1", 1), ("split q", 1), ("query", 0),
     ("copy qk", 2), ("split w", 1), ("query", 1), ("split w", 2), ("project es", 0), ("copy query", 0),
     ("normalise 1", 1), ("copy query", 1), ("copy es", 0), ("score", 2), ("causal", 0), ("mask", 0),
     ("transpose s", 1), ("query", 2), ("exp", 2), ("causal", 1), ("copy query", 2), ("stack s", 1), ("mask", 1),
     ("query", 3), ("sum", 0), ("transpose prob", 2), ("causal", 2), ("copy query", 3), ("copy prob", 2),
     ("mask", 2), ("query", 4), ("sum", 1), ("attend", 2), ("split gate", 0), ("copy query", 4), ("residual 1", 2),
     ("causal", 3), ("project es", 1), ("mask", 3), ("normalise 1", 2), ("query", 5), ("copy es", 1),
     ("causal", 4), ("copy query", 5), ("split w", 3), ("query", 6), ("project qk", 3), ("copy qk", 3), ("sum", 2),
     ("sum", 3), ("copy query", 6), ("transpose s", 2), ("score", 3), ("mask", 4), ("stack s", 2), ("copy sum", 0),
     ("causal", 5), ("query", 7), ("mask", 5), ("sum", 4), ("exp", 3), ("copy query", 7), ("causal", 6),
     ("query", 8), ("sum", 5), ("transpose prob", 3), ("untranspose sum", 0), ("split w", 4), ("mask", 6),
     ("query", 9), ("copy query", 8), ("copy prob", 3), ("causal", 7), ("attend", 3), ("mask", 7), ("query", 10),
     ("causal", 8), ("residual 2", 0), ("residual 1", 3), ("normalise 2", 0), ("copy query", 9),
     ("normalise 1", 3), ("project es", 2), ("sum", 6), ("sum", 7), ("mask", 8), ("copy query", 10),
     ("copy es", 2), ("transpose s", 3), ("causal", 9), ("copy sum", 1), ("untranspose sum", 1), ("stack s", 3),
     ("query", 11), ("residual 2", 1), ("project es", 3), ("normalise 2", 1), ("sum", 8), ("mask", 9),
     ("split w", 5), ("copy es", 3), ("copy query", 11), ("transpose s2", 0), ("stack s2", 0), ("causal", 10),
     ("transpose s2", 1), ("stack s2", 1), ("query", 12), ("sum", 9), ("gate", 0), ("copy query", 12),
     ("mask", 10), ("query", 13), ("split w", 6), ("gate exp", 0), ("gate top", 0), ("causal", 11), ("query", 14),
     ("sum", 10), ("mask", 11), ("causal", 12), ("copy query", 13), ("mask", 12), ("sum", 11), ("copy sum", 2),
     ("gate weights", 0), ("causal", 13), ("transpose weights", 0), ("query", 15), ("copy query", 14),
     ("spread weights", 0), ("sum", 12), ("mask", 13), ("copy query", 15), ("causal", 14), ("sum", 13),
     ("mask", 14), ("causal", 15), ("mask", 15), ("untranspose sum", 2), ("sum", 14), ("up", 0), ("up", 1),
     ("residual 2", 2), ("expert", 0), ("sum", 15), ("expert", 1), ("up", 2), ("up", 3), ("copy sum", 3),
     ("normalise 2", 2), ("untranspose sum", 3), ("expert", 2), ("transpose s2", 2), ("expert", 3), ("up", 4),
     ("residual 2", 3), ("expert", 4), ("up", 5), ("down", 0), ("expert", 5), ("normalise 2", 3), ("stack s2", 2),
     ("up", 6), ("up", 7), ("expert", 6), ("expert", 7), ("down", 1), ("transpose s2", 3), ("stack s2", 3),
     ("up", 8), ("up", 9), ("gate", 1), ("expert", 8), ("expert", 9), ("down", 2), ("down", 3), ("up", 10),
     ("gate exp", 1), ("gate top", 1), ("gate weights", 1), ("up", 11), ("split w", 7), ("down", 4),
     ("transpose weights", 1), ("expert", 10), ("expert", 11), ("up", 12), ("expert", 12), ("up", 13),
     ("spread weights", 1), ("up", 14), ("expert", 13), ("up", 15), ("down", 5), ("expert", 14), ("expert", 15),
     ("up", 16), ("up", 17), ("expert", 16), ("expert", 17), ("down", 6), ("up", 18), ("up", 19), ("expert", 18),
     ("down", 7), ("up", 20), ("expert", 19), ("up", 21), ("expert", 20), ("down", 8), ("up", 22), ("expert", 21),
     ("expert", 22), ("up", 23), ("expert", 23), ("down", 9), ("up", 24), ("up", 25), ("expert", 24),
     ("expert", 25), ("down", 10), ("up", 26), ("expert", 26), ("up", 27), ("expert", 27), ("down", 11),
     ("up", 28), ("up", 29), ("expert", 28), ("down", 12), ("up", 30), ("expert", 29), ("up", 31), ("down", 13),
     ("expert", 30), ("down", 14), ("expert", 31), ("down", 15), ("output", 0), ("output", 1)])

ALL_BANKS, SHARED_BANKS = (6, 7, 0, 1, 2, 3, 4, 5), (6, 7)
USES = {"bias": ["bias"], "transpose x": ["xT"], "project qk": ["q", "k"], "transpose e": ["eT"], "project v": ["v"], "score": ["S"],
        "transpose prob": ["PT"], "attend": ["PV"], "transpose s": ["sT"], "project es": ["es0", "es1"],
        "untranspose sum": ["r"], "transpose s2": ["s2T"], "gate": ["lg"], "transpose weights": ["dT"]}


def misc_turns():
    turns, used = {}, [0] * 8
    at, early, before_output = 0, None, None
    for name, i in SCHEDULE:
        if name == "query" and early is None:
            early, at = list(used), 0
        if name == "output" and before_output is None:
            before_output = list(used)
        for use in USES.get(name, []):
            among = ALL_BANKS if early is None else SHARED_BANKS
            bank = among[at % len(among)]
            used[bank] += 1
            turns[use, i] = (bank, used[bank])
            at += 1
    return turns, early, before_output, used


def hybrid_kernel(nc, x, wq, bq, wk, bk, wv, bv, gamma, Q, E, gate_w, gate_b, w1, w2, w3, d_scratch, out):
    turns, early_uses, uses_before_output, all_uses = misc_turns()
    x_tok = x.rearrange("b h w c -> (b h w) c").rearrange("(t p) c -> p t c", p=P)
    out_tok = out.rearrange("b h w c -> (b h w) c").rearrange("(t p) c -> p t c", p=P)
    NT = IMAGES * TILES

    ctx = ExitStack()
    with ctx:
        def sb(name, shape, dt=FP32):
            return ctx.enter_context(nc.sbuf_tensor(name, shape, dt))

        def sem(name):
            return ctx.enter_context(nc.semaphore(name))

        ident = sb("ident", [P, P])
        twin = sb("twin", [P, C])
        one = sb("one", [1, 1])
        lo_rows = sb("lo_rows", [P, 2])
        neg_half = sb("neg_half", [P, TILES])
        xd = sb("xd", [P, NT, 2, C])
        wqk_in = sb("wqk_in", [P, 2, QK])
        b_in = sb("b_in", [1, 2, QK])
        b_row = sb("b_row", [1, 2, 4, 32])
        wv_in = sb("wv_in", [P, C])
        bv_in = sb("bv_in", [P, C])
        gamma_in = sb("gamma_in", [P, 1])
        q_in = sb("q_in", [P, HEADS, C])
        e_in = sb("e_in", [P, PAIRS, 2, C])
        gate_in = sb("gate_in", [P, EXPERTS])
        gate_b_in = sb("gate_b_in", [P, EXPERTS])
        w_in = sb("w_in", [P, 2, EXPERTS * HIDDEN])
        w3_in = sb("w3_in", [P, EXPERTS, C])
        wqk = [sb(f"wqk_{s}", [P, 2, 4, 32], F32R) for s in ("hi", "lo")]
        wv_gamma = sb("wv_gamma", [P, C])
        bv_gamma = sb("bv_gamma", [P, C])
        wvs = [sb(f"wv_{s}", [P, C], F32R) for s in ("hi", "lo")]
        Qs = [sb(f"Q_{s}", [P, HEADS, 2, C], F32R) for s in ("hi", "lo")]
        Es = [sb(f"E_{s}", [P, HEADS * C], F32R) for s in ("hi", "lo")]
        gates = [sb(f"gate_{s}", [P, EXPERTS], F32R) for s in ("hi", "lo")]
        ws = [sb(f"w_{s}", [P, 2, EXPERTS * HIDDEN], F32R) for s in ("hi", "lo")]
        xT = sb("xT", [P, IMAGES * TOKENS], F32R)
        sT = sb("sT", [P, IMAGES * TOKENS], F32R)
        s2T = sb("s2T", [P, IMAGES * TOKENS], F32R)
        b_col = sb("b_col", [P, 4])
        hi_part = sb("hi_part", [P, 2, 2, TOKENS], F32R)
        qk = sb("qk", [P, 2, 2, TOKENS], F32R)
        v = sb("v", [P, IMAGES, TILES, C + 1])
        nmax = sb("nmax", [P, 2, TILES])
        prob = sb("prob", [P, 2, TILES, TOKENS])
        probT = sb("probT", [P, 2, TILES, TOKENS])
        rsum = sb("rsum", [P, 2, TILES])
        x1 = sb("x1", [P, NT, C])
        x2 = sb("x2", [P, NT, C])
        stats = sb("stats", [P, 2, TILES, 6])
        mv = sb("mv", [P, 2, IMAGES, TILES, 2])
        veps = sb("veps", [P, 2, IMAGES, TILES])
        rstd = sb("rstd", [P, 2, IMAGES, TILES])
        sd = sb("sd", [P, 2, 2, TILES, 2, C])
        es = sb("es", [P, 2, TILES, HEADS * C])
        q_parts = [sb(f"qs_{s}", [P, 2, 2, TOKENS], F32R) for s in ("hi", "lo")]
        omega = sb("omega", [P, OM, 3, 2, P])
        rts = sb("rts", [P, 2, TOKENS])
        lg = sb("lg", [P, HTILES, EXPERTS])
        lmax = sb("lmax", [P, HTILES])
        gp = sb("gp", [P, HTILES, EXPERTS])
        gsum = sb("gsum", [P, HTILES])
        grec = sb("grec", [P, HTILES])
        probs = sb("probs", [P, HTILES, EXPERTS])
        top8 = sb("top8", [P, HTILES, 8])
        rest = sb("rest", [P, HTILES, EXPERTS])
        tsum = sb("tsum", [P, HTILES])
        trec = sb("trec", [P, HTILES])
        dsel = sb("dsel", [P, HTILES, EXPERTS])
        disp = sb("disp", [P, HTILES, EXPERTS])
        dispT = sb("dispT", [HTILES * EXPERTS, HALVES, P])
        dbc = sb("dbc", [P, EXPERTS, HALF])
        sil = sb("sil", [P, SIL, HALF])
        uu = sb("uu", [P, UU, HALF])
        hid = sb("hid", [P, HID, HALF])
        yts = sb("yts", [P, HALVES, HALF])

        banks = [ctx.enter_context(nc.psum_tensor(f"bank{i}", [P, 512], FP32)) for i in range(8)]
        Q_BANK, DIAG_BANK, OFF_BANK, RT_BANK = (0, 1), (2, 3), 4, 5
        U1_BANK, U2_BANK, Y_BANK = (0, 1), (2, 3), (4, 5)

        ld_x0, ld_x = sem("ld_x0"), sem("ld_x")
        ld_wqk, ld_b, ld_wv, ld_bv, ld_q, ld_e = (sem("ld_" + n) for n in ("wqk", "b", "wv", "bv", "q", "e"))
        ld_gate, ld_gate_b, ld_w, ld_w3 = sem("ld_gate"), sem("ld_gate_b"), sem("ld_w"), sem("ld_w3")
        zeroed, consts = sem("zeroed"), sem("consts")
        b_row_ready, wqk_ready, wv_ready = sem("b_row_ready"), sem("wqk_ready"), sem("wv_ready")
        Q_hi_done, Q_ready, gate_ready = sem("Q_hi_done"), sem("Q_ready"), sem("gate_ready")
        w_hi_done, w_ready = sem("w_hi_done"), sem("w_ready")
        E_hi_done, E_lo_done = sem("E_hi_done"), sem("E_lo_done")
        filled = [sem(f"filled{i}") for i in range(8)]
        emptied = [sem(f"emptied{i}") for i in range(8)]
        xT_hi, qk_hi, sT_hi, s2T_hi = sem("xT_hi"), sem("qk_hi"), sem("sT_hi"), sem("s2T_hi")
        nmax_ready = sem("nmax_ready")
        var_ready = [sem("var1_ready"), sem("var2_ready")]
        rstd_ready = [sem("rstd1_ready"), sem("rstd2_ready")]
        sd_ready = [sem("sd1_ready"), sem("sd2_ready")]
        q_filled, qhi_done, qlo_done = sem("q_filled"), sem("qhi_done"), sem("qlo_done")
        diag_filled, off_filled = sem("diag_filled"), sem("off_filled")
        diag_done, off_done, masked = sem("diag_done"), sem("off_done"), sem("masked")
        r_done, rts_done = sem("r_done"), sem("rts_done")
        lg_ready, gexp_done, disp_ready = sem("lg_ready"), sem("gexp_done"), sem("disp_ready")
        d_stored = sem("d_stored")
        dbc_ld = [[sem(f"dbc_ld{h}_{c}") for c in range(4)] for h in range(HALVES)]
        u1_filled, u2_filled, sil_done, uu_done, hid_done, hid_by_dve, down_done = (
            sem(n) for n in ("u1_filled", "u2_filled", "sil_done", "uu_done", "hid_done", "hid_by_dve", "down_done"))
        yts_done, y_filled, res_ready, stored = sem("yts_done"), sem("y_filled"), sem("res_ready"), sem("stored")
        dve_step, pool_step = sem("dve_step"), sem("pool_step")

        def bank_of(use, i):
            return banks[turns[use, i][0]]

        def wait_free(eng, use, i):
            bank, nth = turns[use, i]
            if nth > 1:
                eng.wait_ge(emptied[bank], nth - 1)

        def wait_filled(eng, use, i):
            bank, nth = turns[use, i]
            eng.wait_ge(filled[bank], nth)

        def wait_emptied(eng, use, i):
            bank, nth = turns[use, i]
            eng.wait_ge(emptied[bank], nth)

        def is_filled(use, i):
            return filled[turns[use, i][0]]

        def is_emptied(use, i):
            return emptied[turns[use, i][0]]

        def img(b):
            return slice(b * TOKENS, (b + 1) * TOKENS)

        def tile(t):
            return slice(t * P, (t + 1) * P)

        block = ctx.enter_context(nc.Block())

        @block.sync
        def _(sp):
            def load_x(images, s):
                tiles = slice(TILES * images.start, TILES * images.stop)
                for copy in range(2):
                    sp.dma_start(xd[:, tiles, copy, :], x_tok[:, tiles, :]).then_inc(s, 16)

            def load_halves(dst, src, s):
                for half in range(2):
                    sp.dma_start(dst[C * half:C * (half + 1)], src).then_inc(s, 16)

            load_x(slice(0, 1), ld_x0)
            sp.dma_start(b_in[0:1, 0, :], bq.unsqueeze(0)).then_inc(ld_b, 16)
            sp.dma_start(b_in[0:1, 1, :], bk.unsqueeze(0)).then_inc(ld_b, 16)
            for m, w in enumerate((wq, wk)):
                sp.dma_start(wqk_in[:, m, :], w.unsqueeze(0).to_broadcast([2, C, QK])).then_inc(ld_wqk, 16)
            sp.dma_start(wv_in[:], wv.unsqueeze(0).to_broadcast([2, C, C])).then_inc(ld_wv, 16)
            load_x(slice(1, IMAGES), ld_x)
            load_halves(q_in, Q.rearrange("h i j -> i h j"), ld_q)
            for copy in range(2):
                sp.dma_start(e_in[:, :, copy, :], E.rearrange("(m g) i k -> (g i) m k", g=2)).then_inc(ld_e, 16)
            for m, w in enumerate((w1, w2)):
                load_halves(w_in[:, m, :].rearrange("p (e h) -> p e h", e=EXPERTS), w.rearrange("e c h -> c e h"), ld_w)
            sp.dma_start(gate_in[:], gate_w.unsqueeze(0).to_broadcast([2, C, EXPERTS])).then_inc(ld_gate, 16)
            sp.dma_start(w3_in[:], w3.rearrange("e h c -> h e c")).then_inc(ld_w3, 16)
            for name, i in SCHEDULE:
                if name == "spread weights":
                    wait_emptied(sp, "dT", i)
                    sp.dma_start(d_scratch[i].rearrange("e (t p) -> t e p", p=P), dispT[:, i, :]).then_inc(d_stored, 16)
                    sp.wait_ge(d_stored, 16 * (i + 1))
                    for c in range(4):
                        if i == 1:
                            sp.wait_ge(hid_done, 4 * (c + 1))
                        src = d_scratch[i, 4 * c:4 * (c + 1), :].rearrange("e t -> (e t)").unsqueeze(0)
                        sp.dma_start(dbc[:, 4 * c:4 * (c + 1), :].rearrange("p e t -> p (e t)"),
                                     src.to_broadcast([P, 4 * HALF])).then_inc(dbc_ld[i][c], 16)
                if name == "output":
                    for k in range(0, HTILES, 2):
                        sp.wait_ge(res_ready, HTILES // 2 * i + k // 2 + 1)
                        t = HTILES * i + k
                        sp.dma_start(out_tok[:, t:t + 2, :], x2[:, t:t + 2, :]).then_inc(stored, 16)
            sp.wait_ge(stored, 16 * HALVES * HTILES // 2)

        @block.gpsimd
        def _(pool):
            def wait_step(ins, count=[0]):
                count[0] += 1
                ins.then_inc(pool_step, 1)
                pool.wait_ge(pool_step, count[0])

            pool.memset(ident[:], 0.0).then_inc(zeroed, 1)
            pool.memset(b_row[:], 0.0).then_inc(zeroed, 1)
            for part in wqk:
                pool.memset(part[:].bitcast(FP32), 0.0).then_inc(zeroed, 1)
            pool.wait_ge(zeroed, 4)
            pool.affine_select(out=ident[:], in_=ident[:], compare_op=ALU.not_equal, fill=1.0, base=0,
                               pattern=[[-1, P]], channel_multiplier=1).then_inc(consts, 1)
            pool.memset(one[:], 1.0).then_inc(consts, 1)
            pool.dma_start(gamma_in[:], gamma.unsqueeze(0).to_broadcast([P, 1])).then_inc(ld_bv, 16)
            pool.dma_start(bv_in[:], bv.unsqueeze(0).to_broadcast([P, C])).then_inc(ld_bv, 16)
            pool.memset(v[:, :, :, C:C + 1], 1.0).then_inc(consts, 1)
            pool.memset(neg_half[:], -0.5)
            wait_step(pool.memset(twin[:], 0.0))
            wait_step(pool.affine_select(out=twin[:], in_=twin[:], compare_op=ALU.not_equal, fill=1.0, base=0,
                                         pattern=[[-1, C]], channel_multiplier=1))
            pool.affine_select(out=twin[:], in_=twin[:], compare_op=ALU.not_equal, fill=1.0, base=-C,
                               pattern=[[-1, C]], channel_multiplier=1).then_inc(consts, 1)
            pool.dma_start(gate_b_in[:], gate_b.unsqueeze(0).to_broadcast([P, EXPERTS])).then_inc(ld_gate_b, 16)
            pool.wait_ge(ld_bv, 32)
            pool.wait_ge(ld_wv, 16)
            wait_step(nc.gpsimd.tensor_scalar(wv_gamma[:], wv_in[:], gamma_in[:, 0:1], None, ALU.mult))
            wait_step(nc.gpsimd.tensor_scalar(bv_gamma[:], bv_in[:], gamma_in[:, 0:1], None, ALU.mult))
            wait_step(nc.gpsimd.tensor_copy(wvs[0][:], wv_gamma[:]))
            nc.gpsimd.tensor_tensor(wvs[1][:], wv_gamma[:], wvs[0][:].bitcast(FP32), ALU.subtract).then_inc(wv_ready, 1)

            for name, i in SCHEDULE:
                if name in ("residual 1", "residual 2"):
                    norm = 0 if name == "residual 1" else 1
                    pool.wait_ge(var_ready[norm], i + 1)
                    nc.gpsimd.tensor_tensor(rstd[:, norm, i, :], veps[:, norm, i, :], neg_half[:],
                                            ALU.pow).then_inc(rstd_ready[norm], 1)
                if name == "split q":
                    pool.wait_ge(Q_hi_done, i + 1)
                    heads = slice(4 * i, 4 * (i + 1))
                    nc.gpsimd.tensor_tensor(Qs[1][:, heads], q_in[:, heads].unsqueeze(2).to_broadcast([P, 4, 2, C]),
                                            Qs[0][:, heads].bitcast(FP32), ALU.subtract).then_inc(Q_ready, 1)
                if name == "split gate":
                    pool.wait_ge(ld_gate, 16)
                    wait_step(nc.gpsimd.tensor_copy(gates[0][:], gate_in[:]))
                    nc.gpsimd.tensor_tensor(gates[1][:], gate_in[:], gates[0][:].bitcast(FP32),
                                            ALU.subtract).then_inc(gate_ready, 1)
                if name == "split w":
                    pool.wait_ge(w_hi_done, i + 1)
                    cols = slice(2 * i * HIDDEN, 2 * (i + 1) * HIDDEN)
                    nc.gpsimd.tensor_tensor(ws[1][:, :, cols], w_in[:, :, cols], ws[0][:, :, cols].bitcast(FP32),
                                            ALU.subtract).then_inc(w_ready, 1)
                if name == "mask":
                    pool.wait_ge(diag_done, i + 1)
                    blocks = omega[:, i % OM, 0:2].rearrange("p d h t -> p (d h) t")
                    pool.affine_select(out=blocks, in_=blocks, compare_op=ALU.is_ge, fill=0.0, base=0,
                                       pattern=[[0, 4], [1, P]], channel_multiplier=-1).then_inc(masked, 1)
                if name == "expert" and i < UNITS - 1:
                    half, e = divmod(i, EXPERTS)
                    pool.wait_ge(uu_done, i + 1)
                    if e % 4 == 0:
                        pool.wait_ge(dbc_ld[half][e // 4], 16)
                    if i >= HID:
                        pool.wait_ge(down_done, (i - HID) // 2 + 1)
                    nc.gpsimd.tensor_tensor(hid[:, i % HID], uu[:, i % UU], dbc[:, e, :],
                                            ALU.mult).then_inc(hid_done, 1)

        @block.scalar
        def _(act):
            def hi_part_of(stack, use, b, s):
                wait_filled(act, use, b)
                nc.scalar.activation(stack[:, img(b)], bank_of(use, b)[:, 0:TOKENS], ACT.Copy).then_inc(s, 1)

            for name, i in SCHEDULE:
                if name == "stack x":
                    hi_part_of(xT, "xT", i, xT_hi)
                if name == "stack s":
                    hi_part_of(sT, "sT", i, sT_hi)
                if name == "stack s2":
                    hi_part_of(s2T, "s2T", i, s2T_hi)
                if name == "split e":
                    wait_filled(act, "eT", 0)
                    nc.scalar.activation(Es[0][:], bank_of("eT", 0)[:], ACT.Copy).then_inc(E_hi_done, 1)
                if name == "split q":
                    act.wait_ge(ld_q, 32)
                    heads = slice(4 * i, 4 * (i + 1))
                    nc.scalar.activation(Qs[0][:, heads], q_in[:, heads].unsqueeze(2).to_broadcast([P, 4, 2, C]),
                                         ACT.Copy).then_inc(Q_hi_done, 1)
                if name == "split w":
                    act.wait_ge(ld_w, 64)
                    cols = slice(2 * i * HIDDEN, 2 * (i + 1) * HIDDEN)
                    nc.scalar.activation(ws[0][:, :, cols], w_in[:, :, cols], ACT.Copy).then_inc(w_hi_done, 1)
                if name == "copy qk":
                    for m, use in enumerate("qk"):
                        if i == 0 and m == 0:
                            wait_emptied(act, "bias", 0)
                        wait_filled(act, use, i)
                        if i >= 2:
                            wait_emptied(act, use, i - 2)
                        nc.scalar.activation(hi_part[:, i % 2, m, :], bank_of(use, i)[:, 0:TOKENS], ACT.Identity,
                                             bias=b_col[:, 2 + m:3 + m], scale=lo_rows[:, m:m + 1]).then_inc(qk_hi, 1)
                if name == "exp":
                    act.wait_ge(nmax_ready, i + 1)
                    for k in range(TILES):
                        last = nc.scalar.activation(prob[:, i % 2, k, :], bank_of("S", i)[:, k * TOKENS:(k + 1) * TOKENS],
                                                    ACT.Exp, bias=nmax[:, i % 2, k:k + 1])
                    last.then_inc(is_emptied("S", i), 1)
                if name == "copy prob":
                    wait_filled(act, "PT", i)
                    if i >= 2:
                        wait_filled(act, "PV", i - 2)
                    nc.scalar.activation(probT[:, i % 2].rearrange("p j n -> p (j n)"), bank_of("PT", i)[:],
                                         ACT.Copy).then_inc(is_emptied("PT", i), 1)
                if name == "copy es":
                    if i >= 2:
                        act.wait_ge(r_done, PAIRS * (i - 1))
                    for u in range(TILES):
                        wait_filled(act, f"es{u}", i)
                        nc.scalar.activation(es[:, i % 2, u, :], bank_of(f"es{u}", i)[:],
                                             ACT.Copy).then_inc(is_emptied(f"es{u}", i), 1)
                if name == "copy query":
                    act.wait_ge(q_filled, i + 1)
                    if i >= 2:
                        act.wait_ge(off_filled, i - 1)
                    nc.scalar.activation(q_parts[0][:, i % 2].rearrange("p h t -> p (h t)"), banks[Q_BANK[i % 2]][:],
                                         ACT.Copy).then_inc(qhi_done, 1)
                if name == "mask":
                    act.wait_ge(diag_filled, i + 1)
                    if i >= OM:
                        act.wait_ge(r_done, i - OM + 1)
                    nc.scalar.activation(omega[:, i % OM, 0:2].rearrange("p d h t -> p (d h t)"),
                                         banks[DIAG_BANK[i % 2]][:], ACT.Copy).then_inc(diag_done, 1)
                    act.wait_ge(off_filled, i + 1)
                    nc.scalar.activation(omega[:, i % OM, 2].rearrange("p h t -> p (h t)"),
                                         banks[OFF_BANK][:, 0:2 * P], ACT.Copy).then_inc(off_done, 1)
                if name == "copy sum":
                    act.wait_ge(r_done, PAIRS * (i + 1))
                    if i >= 2:
                        wait_filled(act, "r", i - 2)
                    nc.scalar.activation(rts[:, i % 2, :], banks[RT_BANK][:, 0:TOKENS], ACT.Copy).then_inc(rts_done, 1)
                if name == "gate exp":
                    act.wait_ge(lg_ready, i + 1)
                    nc.scalar.activation(gp[:], lg[:], ACT.Exp).then_inc(gexp_done, 1)
                if name == "spread weights":
                    wait_filled(act, "dT", i)
                    nc.scalar.activation(dispT[:, i, :], bank_of("dT", i)[0:HTILES * EXPERTS, 0:P],
                                         ACT.Copy).then_inc(is_emptied("dT", i), 1)
                if name == "expert":
                    act.wait_ge(u1_filled, i + 1)
                    if i >= SIL:
                        act.wait_ge(uu_done, i - SIL + 1)
                    nc.scalar.activation(sil[:, i % SIL], banks[U1_BANK[i % 2]][:], ACT.Silu).then_inc(sil_done, 1)
                if name == "output":
                    act.wait_ge(down_done, EXPERTS // 2 * (i + 1))
                    for cols in (slice(0, HALF // 2), slice(HALF // 2, HALF)):
                        nc.scalar.activation(yts[:, i, cols], banks[Y_BANK[i]][:, cols], ACT.Copy).then_inc(yts_done, 1)

        @block.vector
        def _(dve):
            def wait_step(ins, count=[0]):
                count[0] += 1
                ins.then_inc(dve_step, 1)
                dve.wait_ge(dve_step, count[0])

            def lo_part_of(stack, use, b, hi_sem):
                dve.wait_ge(hi_sem, b + 1)
                nc.vector.tensor_tensor(stack[C:P, img(b)], bank_of(use, b)[C:P, 0:TOKENS],
                                        stack[C:P, img(b)].bitcast(FP32), ALU.subtract).then_inc(is_emptied(use, b), 1)

            def statistics(norm, b, src):
                for k in range(TILES):
                    last = nc.vector.bn_stats(stats[:, norm, k, :], src[:, TILES * b + k, :])
                wait_step(last)
                for k in range(TILES):
                    last = nc.vector.bn_aggr(mv[:, norm, b, k, :], stats[:, norm, k, :])
                wait_step(last)
                nc.vector.tensor_scalar(veps[:, norm, b, :], mv[:, norm, b, :, 1], EPS, None,
                                        ALU.add).then_inc(var_ready[norm], 1)

            def normalise(norm, b, src):
                dve.wait_ge(rstd_ready[norm], b + 1)
                for k in range(TILES):
                    last = nc.vector.tensor_scalar(
                        sd[:, norm, b % 2, k], src[:, TILES * b + k, :].unsqueeze(1).to_broadcast([P, 2, C]),
                        mv[:, norm, b, k, 0:1], rstd[:, norm, b, k:k + 1], ALU.subtract, ALU.mult)
                last.then_inc(sd_ready[norm], 1)

            wait_step(nc.vector.memset(lo_rows[:], 0.0))
            for rows, m in ((slice(32, 64), 0), (slice(96, 128), 0), (slice(64, 128), 1)):
                wait_step(nc.vector.memset(lo_rows[rows, m:m + 1], 1.0))
            dve.wait_ge(zeroed, 4)
            dve.wait_ge(ld_b, 32)
            nc.vector.tensor_copy(b_row[0:1, :, :, 0:QK],
                                  b_in[0:1].unsqueeze(2).to_broadcast([1, 2, 4, QK])).then_inc(b_row_ready, 1)

            for name, i in SCHEDULE:
                if name == "project qk" and i == 0:
                    dve.wait_ge(ld_wqk, 32)
                    four = [wqk_in[:, m, :].unsqueeze(1).to_broadcast([P, 4, QK]) for m in range(2)]
                    for m in range(2):
                        last = nc.vector.tensor_copy(wqk[0][:, m, :, 0:QK], four[m])
                    wait_step(last)
                    for m in range(2):
                        last = nc.vector.tensor_tensor(wqk[1][:, m, :, 0:QK], four[m],
                                                       wqk[0][:, m, :, 0:QK].bitcast(FP32), ALU.subtract)
                    last.then_inc(wqk_ready, 1)
                if name == "bias":
                    wait_filled(dve, "bias", 0)
                    wait_step(nc.vector.tensor_copy(b_col[:, 0:2], bank_of("bias", 0)[:, 0:2]))
                    nc.vector.tensor_tensor(b_col[:, 2:4], b_col[:, 0:2], lo_rows[:],
                                            ALU.mult).then_inc(is_emptied("bias", 0), 1)
                if name == "stack x":
                    lo_part_of(xT, "xT", i, xT_hi)
                if name == "stack s":
                    lo_part_of(sT, "sT", i, sT_hi)
                if name == "stack s2":
                    lo_part_of(s2T, "s2T", i, s2T_hi)
                if name == "split e":
                    dve.wait_ge(E_hi_done, 1)
                    nc.vector.tensor_tensor(Es[1][:], bank_of("eT", 0)[:], Es[0][:].bitcast(FP32),
                                            ALU.subtract).then_inc(is_emptied("eT", 0), 1)
                if name == "copy qk":
                    for m, use in enumerate("qk"):
                        if i == 0 and m == 0:
                            wait_emptied(dve, "bias", 0)
                        dve.wait_ge(qk_hi, 2 * i + m + 1)
                        nc.vector.scalar_tensor_tensor(out=qk[:, i % 2, m, :], in0=bank_of(use, i)[:, 0:TOKENS],
                                                       scalar=b_col[:, m:m + 1], in1=hi_part[:, i % 2, m, :].bitcast(FP32),
                                                       op0=ALU.add, op1=ALU.subtract).then_inc(is_emptied(use, i), 1)
                if name == "copy v":
                    wait_filled(dve, "v", i)
                    if i == 0:
                        dve.wait_ge(consts, 3)
                        dve.wait_ge(wv_ready, 1)
                    nc.vector.tensor_tensor(v[:, i, :, 0:C],
                                            bank_of("v", i)[:, 0:TILES * C].rearrange("p (k c) -> p k c", k=TILES),
                                            bv_gamma[:].unsqueeze(1).to_broadcast([P, TILES, C]),
                                            ALU.add).then_inc(is_emptied("v", i), 1)
                if name == "exp":
                    wait_filled(dve, "S", i)
                    nc.vector.tensor_reduce(nmax[:, i % 2, :],
                                            bank_of("S", i)[:].rearrange("p (k m) -> p k m", k=TILES), AX.X, ALU.max,
                                            negate=True).then_inc(nmax_ready, 1)
                if name == "residual 1":
                    wait_filled(dve, "PV", i)
                    pv = bank_of("PV", i)[:, 0:TILES * (C + 1)].rearrange("p (k c) -> p k c", k=TILES)
                    wait_step(nc.vector.reciprocal(rsum[:, i % 2, :], pv[:, :, C]))
                    for k in range(TILES):
                        last = nc.vector.scalar_tensor_tensor(
                            out=x1[:, TILES * i + k, :], in0=pv[:, k, 0:C], scalar=rsum[:, i % 2, k:k + 1],
                            in1=xd[:, TILES * i + k, 0, :], op0=ALU.mult, op1=ALU.add)
                    last.then_inc(is_emptied("PV", i), 1)
                    wait_emptied(dve, "PV", i)
                    statistics(0, i, x1)
                if name == "normalise 1":
                    normalise(0, i, x1)
                if name == "copy query":
                    dve.wait_ge(qhi_done, i + 1)
                    nc.vector.tensor_tensor(q_parts[1][:, i % 2].rearrange("p h t -> p (h t)"), banks[Q_BANK[i % 2]][:],
                                            q_parts[0][:, i % 2].rearrange("p h t -> p (h t)").bitcast(FP32),
                                            ALU.subtract).then_inc(qlo_done, 1)
                if name == "residual 2":
                    wait_filled(dve, "r", i)
                    nc.vector.tensor_tensor(x2[:, TILES * i:TILES * (i + 1), :], x1[:, TILES * i:TILES * (i + 1), :],
                                            bank_of("r", i)[:, 0:TILES * C].rearrange("p (k c) -> p k c", k=TILES),
                                            ALU.add).then_inc(is_emptied("r", i), 1)
                    wait_emptied(dve, "r", i)
                    statistics(1, i, x2)
                if name == "normalise 2":
                    normalise(1, i, x2)
                spread = [P, HTILES, EXPERTS]
                if name == "gate exp":
                    wait_filled(dve, "lg", i)
                    if i == 0:
                        dve.wait_ge(ld_gate_b, 16)
                    lg_psum = bank_of("lg", i)[:, 0:HTILES * EXPERTS].rearrange("p (t e) -> p t e", t=HTILES)
                    nc.vector.tensor_tensor(lg[:], lg_psum, gate_b_in[:].unsqueeze(1).to_broadcast(spread),
                                            ALU.add).then_inc(is_emptied("lg", i), 1)
                    wait_emptied(dve, "lg", i)
                    wait_step(nc.vector.tensor_reduce(lmax[:], lg[:], AX.X, ALU.max))
                    nc.vector.tensor_tensor(lg[:], lg[:], lmax[:].unsqueeze(2).to_broadcast(spread),
                                            ALU.subtract).then_inc(lg_ready, 1)
                if name == "gate top":
                    dve.wait_ge(gexp_done, i + 1)
                    wait_step(nc.vector.tensor_reduce(gsum[:], gp[:], AX.X, ALU.add))
                    wait_step(nc.vector.reciprocal(grec[:], gsum[:]))
                    wait_step(nc.vector.tensor_tensor(probs[:], gp[:], grec[:].unsqueeze(2).to_broadcast(spread), ALU.mult))
                    for t in range(HTILES):
                        last = nc.vector.max(top8[:, t, :], probs[:, t, :])
                    wait_step(last)
                    wait_step(nc.vector.tensor_tensor(tsum[:], top8[:, :, 0], top8[:, :, 1], ALU.add))
                if name == "gate weights":
                    nc.vector.reciprocal(trec[:], tsum[:])
                    wait_step(nc.vector.memset(top8[:, :, 2:8], -1.0))
                    for t in range(HTILES):
                        last = nc.vector.match_replace(out=rest[:, t, :], in_to_replace=top8[:, t, :],
                                                       in_values=probs[:, t, :], imm_value=0.0)
                    wait_step(last)
                    wait_step(nc.vector.tensor_tensor(dsel[:], probs[:], rest[:], ALU.subtract))
                    nc.vector.tensor_tensor(disp[:], dsel[:], trec[:].unsqueeze(2).to_broadcast(spread),
                                            ALU.mult).then_inc(disp_ready, 1)
                if name == "expert":
                    dve.wait_ge(u2_filled, i + 1)
                    dve.wait_ge(sil_done, i + 1)
                    if i >= UU:
                        dve.wait_ge(hid_done, i - UU + 1)
                    nc.vector.tensor_tensor(uu[:, i % UU], banks[U2_BANK[i % 2]][:], sil[:, i % SIL],
                                            ALU.mult).then_inc(uu_done, 1)
                    if i == UNITS - 1:
                        dve.wait_ge(uu_done, UNITS)
                        dve.wait_ge(down_done, (i - HID) // 2 + 1)
                        nc.vector.tensor_tensor(hid[:, i % HID], uu[:, i % UU], dbc[:, i % EXPERTS, :],
                                                ALU.mult).then_inc(hid_by_dve, 1)
                if name == "output":
                    for k in range(0, HTILES, 2):
                        t = HTILES * i + k
                        dve.wait_ge(y_filled, HTILES // 2 * i + k // 2 + 1)
                        nc.vector.tensor_tensor(x2[:, t:t + 2, :], x2[:, t:t + 2, :],
                                                banks[6 + k // 2][:, 0:2 * C].rearrange("p (t c) -> p t c", t=2),
                                                ALU.add).then_inc(res_ready, 1)

        @block.tensor
        def _(pe):
            def two_pass(dst, weights, moving):
                nc.tensor.matmul(dst, weights[0], moving[0], start=True, stop=False)
                return nc.tensor.matmul(dst, weights[1], moving[1], start=False, stop=True)

            def transpose_tiles(use, b, tiles):
                wait_free(pe, use, b)
                for k, src in enumerate(tiles):
                    last = nc.tensor.transpose(bank_of(use, b)[:, tile(k)], src, ident[:])
                last.then_inc(is_filled(use, b), 1)

            for name, i in SCHEDULE:
                if name == "bias":
                    pe.wait_ge(consts, 2)
                    pe.wait_ge(b_row_ready, 1)
                    for m in range(2):
                        last = nc.tensor.matmul(bank_of("bias", 0)[:, m:m + 1], b_row[0:1, m].rearrange("o g n -> o (g n)"),
                                                one[0:1, 0:1], start=True, stop=True)
                    last.then_inc(is_filled("bias", 0), 1)
                if name == "transpose x":
                    if i == 0:
                        pe.wait_ge(consts, 1)
                    pe.wait_ge(ld_x0 if i == 0 else ld_x, 32)
                    transpose_tiles("xT", i, [xd[:, TILES * i + k].rearrange("p d c -> p (d c)") for k in range(TILES)])
                if name == "transpose e":
                    pe.wait_ge(ld_e, 32)
                    transpose_tiles("eT", i, [e_in[:, m].rearrange("p d k -> p (d k)") for m in range(PAIRS)])
                if name == "project qk":
                    if i == 0:
                        pe.wait_ge(wqk_ready, 1)
                    wait_emptied(pe, "xT", i)
                    for m, use in enumerate("qk"):
                        wait_free(pe, use, i)
                        two_pass(bank_of(use, i)[:, 0:TOKENS], [part[:, m].rearrange("p g n -> p (g n)") for part in wqk],
                                 [xT[:, img(i)]] * 2).then_inc(is_filled(use, i), 1)
                if name == "project v":
                    if i == 0:
                        pe.wait_ge(wv_ready, 1)
                    wait_emptied(pe, "xT", i)
                    wait_free(pe, "v", i)
                    for k in range(TILES):
                        last = two_pass(bank_of("v", i)[:, C * k:C * (k + 1)], [xT[:, tile(TILES * i + k)]] * 2,
                                        [part[:] for part in wvs])
                    last.then_inc(is_filled("v", i), 1)
                if name == "score":
                    wait_emptied(pe, "q", i)
                    wait_emptied(pe, "k", i)
                    wait_free(pe, "S", i)
                    for k in range(TILES):
                        last = nc.tensor.matmul(bank_of("S", i)[:, k * TOKENS:(k + 1) * TOKENS], qk[:, i % 2, 0, tile(k)],
                                                qk[:, i % 2, 1, :], start=True, stop=True)
                    last.then_inc(is_filled("S", i), 1)
                if name == "transpose prob":
                    wait_emptied(pe, "S", i)
                    transpose_tiles("PT", i, [prob[:, i % 2, k, tile(j)] for j in range(TILES) for k in range(TILES)])
                if name == "attend":
                    wait_emptied(pe, "PT", i)
                    wait_emptied(pe, "v", i)
                    wait_free(pe, "PV", i)
                    for k in range(TILES):
                        for j in range(TILES):
                            last = nc.tensor.matmul(bank_of("PV", i)[:, (C + 1) * k:(C + 1) * (k + 1)],
                                                    probT[:, i % 2, j, tile(k)], v[:, i, j, :],
                                                    start=(j == 0), stop=(j == TILES - 1))
                    last.then_inc(is_filled("PV", i), 1)
                if name == "transpose s":
                    pe.wait_ge(sd_ready[0], i + 1)
                    transpose_tiles("sT", i, [sd[:, 0, i % 2, k].rearrange("p d c -> p (d c)") for k in range(TILES)])
                if name == "project es":
                    if i == 0:
                        wait_emptied(pe, "eT", 0)
                    wait_emptied(pe, "sT", i)
                    for u in range(TILES):
                        use = f"es{u}"
                        wait_free(pe, use, i)
                        two_pass(bank_of(use, i)[:], [sT[:, tile(TILES * i + u)]] * 2,
                                 [part[:] for part in Es]).then_inc(is_filled(use, i), 1)
                b, pair = divmod(i, PAIRS)
                if name == "query":
                    if i == 0:
                        for bank in (*Q_BANK, *DIAG_BANK, OFF_BANK, RT_BANK):
                            pe.wait_ge(emptied[bank], early_uses[bank])
                    if pair == 0:
                        wait_emptied(pe, "sT", b)
                    if b == 0:
                        pe.wait_ge(Q_ready, 1 + pair // 2)
                    if i >= 2:
                        pe.wait_ge(qlo_done, i - 1)
                    for hh in range(2):
                        h = 2 * pair + hh
                        last = two_pass(banks[Q_BANK[i % 2]][:, hh * TOKENS:(hh + 1) * TOKENS],
                                        [part[:, h].rearrange("p d j -> p (d j)") for part in Qs], [sT[:, img(b)]] * 2)
                    last.then_inc(q_filled, 1)
                if name == "causal":
                    pe.wait_ge(qlo_done, i + 1)
                    u = [sT[:, tile(TILES * b + k)] for k in range(TILES)]
                    at = [[part[:, i % 2, :, tile(k)] for part in q_parts] for k in range(TILES)]
                    if i >= 2:
                        pe.wait_ge(diag_done, i - 1)
                    two_pass(banks[DIAG_BANK[i % 2]][:, 0:2 * P], [u[0]] * 2, at[0])
                    two_pass(banks[DIAG_BANK[i % 2]][:, 2 * P:4 * P], [u[1]] * 2, at[1]).then_inc(diag_filled, 1)
                    if i >= 1:
                        pe.wait_ge(off_done, i)
                    two_pass(banks[OFF_BANK][:, 0:2 * P], [u[0]] * 2, at[1]).then_inc(off_filled, 1)
                if name == "sum":
                    pe.wait_ge(off_done, i + 1)
                    pe.wait_ge(masked, i + 1)
                    if pair == 0:
                        wait_emptied(pe, "es0", b)
                        wait_emptied(pe, "es1", b)
                        if b >= 1:
                            pe.wait_ge(rts_done, b)
                    for u in range(2):
                        for hh in range(2):
                            h = 2 * pair + hh
                            blocks = omega[:, i % OM, 0:3:2, hh, :] if u == 0 else omega[:, i % OM, 1, hh, :]
                            last = nc.tensor.matmul(banks[RT_BANK][C * hh:C * (hh + 1), P * u:TOKENS],
                                                    es[:, b % 2, u, C * h:C * (h + 1)], blocks,
                                                    start=(pair == 0 and u == 0), stop=(pair == PAIRS - 1 and u == 1))
                    last.then_inc(r_done, 1)
                if name == "untranspose sum":
                    if i == 0:
                        pe.wait_ge(consts, 4)
                    pe.wait_ge(rts_done, i + 1)
                    wait_free(pe, "r", i)
                    for k in range(TILES):
                        last = nc.tensor.matmul(bank_of("r", i)[:, C * k:C * (k + 1)], rts[:, i % 2, tile(k)], twin[:],
                                                start=True, stop=True)
                    last.then_inc(is_filled("r", i), 1)
                if name == "transpose s2":
                    pe.wait_ge(sd_ready[1], i + 1)
                    transpose_tiles("s2T", i, [sd[:, 1, i % 2, k].rearrange("p d c -> p (d c)") for k in range(TILES)])
                if name == "gate":
                    if i == 0:
                        pe.wait_ge(gate_ready, 1)
                    wait_emptied(pe, "s2T", 2 * i)
                    wait_emptied(pe, "s2T", 2 * i + 1)
                    wait_free(pe, "lg", i)
                    for t in range(HTILES):
                        last = two_pass(bank_of("lg", i)[:, EXPERTS * t:EXPERTS * (t + 1)],
                                        [s2T[:, tile(HTILES * i + t)]] * 2, [part[:] for part in gates])
                    last.then_inc(is_filled("lg", i), 1)
                if name == "transpose weights":
                    pe.wait_ge(disp_ready, i + 1)
                    wait_free(pe, "dT", i)
                    nc.tensor.transpose(bank_of("dT", i)[0:HTILES * EXPERTS, 0:P], disp[:].rearrange("p t e -> p (t e)"),
                                        ident[:]).then_inc(is_filled("dT", i), 1)
                if name == "up":
                    half, e = divmod(i, EXPERTS)
                    if e == 0:
                        wait_emptied(pe, "s2T", 2 * half)
                        wait_emptied(pe, "s2T", 2 * half + 1)
                    if i < EXPERTS and e % 2 == 0:
                        pe.wait_ge(w_ready, e // 2 + 1)
                    if i < 2:
                        pe.wait_ge(qlo_done, IMAGES * PAIRS - 1 + i)
                        pe.wait_ge(diag_done, IMAGES * PAIRS - 1 + i)
                    else:
                        pe.wait_ge(uu_done, i - 1)
                    moving = s2T[:, half * HALF:(half + 1) * HALF]
                    for m, (bank, full) in enumerate(((U1_BANK, u1_filled), (U2_BANK, u2_filled))):
                        two_pass(banks[bank[i % 2]][:], [part[:, m, HIDDEN * e:HIDDEN * (e + 1)] for part in ws],
                                 [moving] * 2).then_inc(full, 1)
                if name == "down":
                    half, e = divmod(2 * i, EXPERTS)
                    if i == 0:
                        pe.wait_ge(ld_w3, 16)
                        pe.wait_ge(off_done, IMAGES * PAIRS)
                    if i == EXPERTS // 2:
                        pe.wait_ge(rts_done, IMAGES)
                    if i == UNITS // 2 - 1:
                        pe.wait_ge(hid_done, UNITS - 1)
                        pe.wait_ge(hid_by_dve, 1)
                    else:
                        pe.wait_ge(hid_done, 2 * i + 2)
                    for n in range(2):
                        last = nc.tensor.matmul(banks[Y_BANK[half]][C * n:C * (n + 1), :], w3_in[:, e + n, :],
                                                hid[:, (2 * i + n) % HID], start=(e == 0), stop=(e == EXPERTS - 2))
                    last.then_inc(down_done, 1)
                if name == "output":
                    for k in range(0, HTILES, 2):
                        pe.wait_ge(yts_done, HTILES // 2 * i + k // 2 + 1)
                        bank = SHARED_BANKS[k // 2]
                        pe.wait_ge(emptied[bank], all_uses[bank] if i == HALVES - 1 else uses_before_output[bank])
                        if i >= 1:
                            pe.wait_ge(res_ready, HTILES // 2 * (i - 1) + k // 2 + 1)
                        for t in range(k, k + 2):
                            last = nc.tensor.matmul(banks[bank][:, C * (t - k):C * (t - k + 1)], yts[:, i, tile(t)],
                                                    twin[:], start=True, stop=True)
                        last.then_inc(y_filled, 1)


_INS = ["x", "L0_conv_wq", "L0_conv_bq", "L0_conv_wk", "L0_conv_bk", "L0_conv_wv", "L0_conv_bv", "L0_conv_gamma",
        "L1_attn_Q", "L1_attn_E", "L1_ffn_gate_w", "L1_ffn_gate_b", "L1_ffn_w1", "L1_ffn_w2", "L1_ffn_w3"]
_OUT = ((4, 16, 16, 64), "float32")


def kernel(**inputs):
    import numpy as _np
    import concourse.bacc as _bacc
    from concourse import mybir as _mybir
    from concourse.bass_utils import run_bass_kernel_spmd as _run

    nc = _bacc.Bacc("TRN2", target_bir_lowering=False, num_devices=1)
    arrays, args = {}, []
    for name in _INS:
        a = _np.ascontiguousarray(inputs[name])
        if a.ndim == 0:
            a = a.reshape(1)
        arrays[f"in_{name}"] = a
        args.append(nc.dram_tensor(f"in_{name}", a.shape, _mybir.dt.from_np(a.dtype), kind="ExternalInput").ap())
    scratch = nc.dram_tensor("dispatch_scratch", (HALVES, EXPERTS, HALF), _mybir.dt.float32).ap()
    shape, dtype = _OUT
    out = nc.dram_tensor("out", shape, _mybir.dt.from_np(_np.dtype(dtype)), kind="ExternalOutput").ap()
    hybrid_kernel(nc, *args, scratch, out)
    result = _run(nc, [arrays], core_ids=[0])
    return result.results[0]["out"]
```

```python
import concourse.bass as bass
from concourse import mybir
from contextlib import ExitStack

FP32 = mybir.dt.float32
F32R = mybir.dt.float32r
ALU = mybir.AluOpType
ACT = mybir.ActivationFunctionType
AX = mybir.AxisListType

P = 128
IMAGES = 4
TOKENS = 256
TILES = TOKENS // P
C = 64
EPS = 1e-5
QK = 8
HEADS = 8
PAIRS = HEADS // 2
EXPERTS = 16
HIDDEN = 128
HALVES = 2
HALF = IMAGES * TOKENS // HALVES
HTILES = HALF // P
UNITS = HALVES * EXPERTS
QS, OM, SIL, UU, HID = 3, 4, 3, 4, 8

CHUNKS = (0, 2, 4, 8, 12, 16)


def chunk_of(expert):
    return sum(expert >= start for start in CHUNKS[1:])


def on_dve(unit):
    return unit % 4 == 3


SCHEDULE = (
    [("transpose x", 0), ("stack x", 0), ("project qk", 0), ("bias", 0), ("transpose x", 1), ("transpose x", 2),
     ("transpose x", 3), ("copy qk", 0), ("stack x", 1), ("project v", 0), ("stack x", 2), ("score", 0),
     ("stack x", 3), ("exp", 0), ("project qk", 1), ("copy v", 0), ("project v", 1), ("copy v", 1),
     ("project qk", 2), ("project v", 2), ("project v", 3), ("copy v", 2), ("copy qk", 1), ("transpose prob", 0),
     ("score", 1), ("copy qk", 2), ("score", 2), ("copy prob", 0), ("exp", 1), ("exp", 2), ("attend", 0),
     ("residual 1", 0), ("copy v", 3), ("split q", 0), ("transpose e", 0), ("transpose prob", 1),
     ("normalise 1", 0), ("split e", 0), ("split q", 1), ("copy prob", 1), ("transpose prob", 2), ("copy prob", 2),
     ("transpose s", 0), ("stack s", 0), ("attend", 1), ("residual 1", 1), ("query", 0), ("split w", 0),
     ("query", 1), ("project es", 0), ("copy query", 0), ("copy es", 0), ("causal", 0), ("normalise 1", 1),
     ("copy query", 1), ("query", 2), ("attend", 2), ("mask", 0), ("copy query", 2), ("transpose s", 1),
     ("causal", 1), ("stack s", 1), ("query", 3), ("sum", 0), ("mask", 1), ("query", 4), ("residual 1", 2),
     ("project qk", 3), ("copy query", 3), ("copy qk", 3), ("causal", 2), ("sum", 1), ("project es", 1),
     ("copy query", 4), ("mask", 2), ("normalise 1", 2), ("query", 5), ("copy es", 1), ("copy query", 5),
     ("causal", 3), ("score", 3), ("sum", 2), ("transpose s", 2), ("mask", 3), ("causal", 4), ("exp", 3),
     ("query", 6), ("sum", 3), ("mask", 4), ("stack s", 2), ("copy sum", 0), ("transpose prob", 3), ("query", 7),
     ("causal", 5), ("split w", 1), ("sum", 4), ("copy query", 6), ("copy prob", 3), ("copy query", 7),
     ("untranspose sum", 0), ("mask", 5), ("attend", 3), ("causal", 6), ("query", 8), ("split w", 2), ("mask", 6),
     ("residual 2", 0), ("residual 1", 3), ("sum", 5), ("split gate", 0), ("causal", 7), ("query", 9),
     ("copy query", 8), ("normalise 2", 0), ("mask", 7), ("split w", 3), ("normalise 1", 3), ("project es", 2),
     ("query", 10), ("sum", 6), ("copy es", 2), ("transpose s", 3), ("sum", 7), ("copy query", 9), ("stack s", 3),
     ("copy query", 10), ("copy sum", 1), ("transpose s2", 0), ("stack s2", 0), ("causal", 8),
     ("untranspose sum", 1), ("query", 11), ("query", 12), ("mask", 8), ("residual 2", 1), ("causal", 9),
     ("copy query", 11), ("mask", 9), ("project es", 3), ("causal", 10), ("normalise 2", 1), ("sum", 8),
     ("copy es", 3), ("transpose s2", 1), ("copy query", 12), ("mask", 10), ("query", 13), ("stack s2", 1),
     ("causal", 11), ("copy query", 13), ("query", 14), ("gate", 0), ("sum", 9), ("mask", 11), ("split w", 4),
     ("gate exp", 0), ("query", 15), ("gate top", 0), ("copy query", 14), ("causal", 12), ("gate weights", 0),
     ("mask", 12), ("sum", 10), ("copy query", 15), ("causal", 13), ("mask", 13), ("sum", 11), ("causal", 14),
     ("copy sum", 2), ("transpose weights", 0), ("split w", 5), ("sum", 12), ("spread weights", 0), ("mask", 14),
     ("causal", 15), ("sum", 13), ("mask", 15), ("untranspose sum", 2), ("residual 2", 2), ("up", 0),
     ("expert", 0), ("up", 1), ("sum", 14), ("up", 2), ("expert", 1), ("up", 3), ("sum", 15), ("expert", 2),
     ("up", 4), ("normalise 2", 2), ("expert", 3), ("copy sum", 3), ("untranspose sum", 3), ("expert", 4),
     ("transpose s2", 2), ("up", 5), ("up", 6), ("residual 2", 3), ("expert", 5), ("expert", 6), ("down", 0),
     ("up", 7), ("split w", 6), ("up", 8), ("normalise 2", 3), ("transpose s2", 3), ("expert", 7), ("stack s2", 2),
     ("up", 9), ("stack s2", 3), ("down", 1), ("expert", 8), ("expert", 9), ("gate", 1), ("gate exp", 1),
     ("down", 2), ("up", 10), ("gate top", 1), ("up", 11), ("down", 3), ("split w", 7), ("expert", 10),
     ("expert", 11), ("gate weights", 1), ("down", 4), ("up", 12), ("up", 13), ("down", 5),
     ("transpose weights", 1), ("expert", 12), ("up", 14), ("expert", 13), ("spread weights", 1), ("up", 15),
     ("expert", 14), ("up", 16), ("expert", 15), ("up", 17), ("down", 6), ("expert", 16), ("expert", 17),
     ("up", 18), ("up", 19), ("down", 7), ("expert", 18), ("expert", 19), ("up", 20), ("up", 21), ("expert", 20),
     ("down", 8), ("up", 22), ("expert", 21), ("expert", 22), ("up", 23), ("expert", 23), ("down", 9), ("up", 24),
     ("expert", 24), ("up", 25), ("down", 10), ("up", 26), ("expert", 25), ("up", 27), ("down", 11),
     ("expert", 26), ("expert", 27), ("up", 28), ("expert", 28), ("up", 29), ("expert", 29), ("down", 12),
     ("output", 0), ("up", 30), ("down", 13), ("down", 14), ("expert", 30), ("up", 31), ("gather", 0),
     ("expert", 31), ("last experts", 0), ("last experts", 1)])

ALL_BANKS, SHARED_BANKS = (6, 7, 0, 1, 2, 3, 4, 5), (6, 7)
USES = {"bias": ["bias"], "transpose x": ["xT"], "project qk": ["q", "k"], "transpose e": ["eT"], "project v": ["v"],
        "score": ["S"], "transpose prob": ["PT"], "attend": ["PV"], "transpose s": ["sT"], "project es": ["es0", "es1"],
        "untranspose sum": ["r"], "transpose s2": ["s2T"], "gate": ["lg"], "transpose weights": ["dT"]}


def misc_turns():
    turns, used = {}, [0] * 8
    at, early, before_output = 0, None, None
    for name, i in SCHEDULE:
        if name == "query" and early is None:
            early, at = list(used), 0
        if name == "output" and before_output is None:
            before_output = list(used)
        for use in USES.get(name, []):
            among = ALL_BANKS if early is None else SHARED_BANKS
            bank = among[at % len(among)]
            used[bank] += 1
            turns[use, i] = (bank, used[bank])
            at += 1
    return turns, early, before_output, used


def hybrid_kernel(nc, x, wq, bq, wk, bk, wv, bv, gamma, Q, E, gate_w, gate_b, w1, w2, w3, d_scratch, out):
    turns, early_uses, uses_before_output, all_uses = misc_turns()
    x_tok = x.rearrange("b h w c -> (b h w) c").rearrange("(t p) c -> p t c", p=P)
    out_tok = out.rearrange("b h w c -> (b h w) c").rearrange("(t p) c -> p t c", p=P)
    NT = IMAGES * TILES

    ctx = ExitStack()
    with ctx:
        def sb(name, shape, dt=FP32):
            return ctx.enter_context(nc.sbuf_tensor(name, shape, dt))

        def sem(name):
            return ctx.enter_context(nc.semaphore(name))

        ident = sb("ident", [P, P])
        twin = sb("twin", [P, C])
        lo_rows = sb("lo_rows", [P, 2])
        neg_half = sb("neg_half", [P, TILES])
        x_in = sb("x_in", [P, NT, C])
        wqk_in = sb("wqk_in", [P, 2, QK])
        b_in = sb("b_in", [1, 2, QK])
        b_row = sb("b_row", [1, 2, 4, 32])
        wv_in = sb("wv_in", [P, C])
        bv_in = sb("bv_in", [P, C])
        gamma_in = sb("gamma_in", [P, 1])
        q_in = sb("q_in", [C, HEADS, C])
        e_in = sb("e_in", [P, PAIRS, C])
        gate_in = sb("gate_in", [P, EXPERTS])
        gate_b_in = sb("gate_b_in", [P, EXPERTS])
        w_in = sb("w_in", [P, 2, EXPERTS * HIDDEN])
        w3_in = sb("w3_in", [P, EXPERTS, C])
        wqk = [sb(f"wqk_{s}", [P, 2, 4, 32], F32R) for s in ("hi", "lo")]
        wv_gamma = sb("wv_gamma", [P, C])
        bv_gamma = sb("bv_gamma", [P, C])
        wvs = sb("wv_parts", [P, 2, C], F32R)
        Qs = sb("Q_stack", [P, HEADS, C], F32R)
        Es = sb("E_stack", [P, HEADS * C], F32R)
        gates = sb("gate_parts", [P, 2, EXPERTS], F32R)
        v_part = sb("v_part", [P, IMAGES, TILES, C])
        lg_part = sb("lg_part", [P, HALVES, HTILES, EXPERTS])
        ws = [sb(f"w_{s}", [P, 2, EXPERTS * HIDDEN], F32R) for s in ("hi", "lo")]
        xT = sb("xT", [P, IMAGES * TOKENS], F32R)
        s_parts = [sb(f"s_{s}", [P, IMAGES * TOKENS], F32R) for s in ("hi", "lo")]
        s2T = sb("s2T", [P, IMAGES * TOKENS], F32R)
        b_col = sb("b_col", [P, 4])
        hi_part = sb("hi_part", [P, 2, 2, TOKENS], F32R)
        qk = sb("qk", [P, 2, 2, TOKENS], F32R)
        v = sb("v", [P, IMAGES, TILES, C + 1])
        nmax = sb("nmax", [P, 2, TILES])
        prob = sb("prob", [P, 2, TILES, TOKENS])
        probT = sb("probT", [P, 2, TILES, TOKENS])
        rsum = sb("rsum", [P, 2, TILES])
        x1 = sb("x1", [P, NT, C])
        x2 = sb("x2", [P, NT, C])
        stats = sb("stats", [P, 2, TILES, 6])
        mv = sb("mv", [P, 2, IMAGES, TILES, 2])
        veps = sb("veps", [P, 2, IMAGES, TILES])
        rstd = sb("rstd", [P, 2, IMAGES, TILES])
        sd = sb("sd", [P, 2, TILES, 2, C])
        s2 = sb("s2", [P, 2, TILES, C])
        es = sb("es", [P, 2, TILES, HEADS * C])
        q_stack = sb("q_stack", [P, QS, 2, TOKENS], F32R)
        omega = sb("omega", [P, OM, 3, 2, P])
        rts = sb("rts", [P, 2, TOKENS])
        lg = sb("lg", [P, HTILES, EXPERTS])
        lmax = sb("lmax", [P, HTILES])
        gp = sb("gp", [P, HTILES, EXPERTS])
        gsum = sb("gsum", [P, HTILES])
        grec = sb("grec", [P, HTILES])
        probs = sb("probs", [P, HTILES, EXPERTS])
        top8 = sb("top8", [P, HTILES, 8])
        rest = sb("rest", [P, HTILES, EXPERTS])
        tsum = sb("tsum", [P, HTILES])
        trec = sb("trec", [P, HTILES])
        dsel = sb("dsel", [P, HTILES, EXPERTS])
        disp = sb("disp", [P, HTILES, EXPERTS])
        dispT = sb("dispT", [HTILES * EXPERTS, HALVES, P])
        dbc = sb("dbc", [P, EXPERTS, HALF])
        sil = sb("sil", [P, SIL, HALF])
        uu = sb("uu", [P, UU, HALF])
        hid = sb("hid", [P, HID, HALF])
        yts = sb("yts", [P, HALVES, HALF])

        banks = [ctx.enter_context(nc.psum_tensor(f"bank{i}", [P, 512], FP32)) for i in range(8)]
        Q_BANK, DIAG_BANK, OFF_BANK, RT_BANK = (0, 1), (2, 3), 4, 5
        U1_BANK, U2_BANK, Y_BANK = (0, 1), (2, 3), (4, 5)

        ld_x0, ld_x = sem("ld_x0"), sem("ld_x")
        ld_wqk, ld_b, ld_wv, ld_bv, ld_q, ld_e = (sem("ld_" + n) for n in ("wqk", "b", "wv", "bv", "q", "e"))
        ld_gate, ld_gate_b, ld_w, ld_w3 = sem("ld_gate"), sem("ld_gate_b"), sem("ld_w"), sem("ld_w3")
        zeroed, consts = sem("zeroed"), sem("consts")
        b_row_ready, wqk_ready, wv_ready = sem("b_row_ready"), sem("wqk_ready"), sem("wv_ready")
        Q_hi_done, Q_ready, gate_ready = sem("Q_hi_done"), sem("Q_ready"), sem("gate_ready")
        w_hi_done, w_hi_by_dve, w_ready = sem("w_hi_done"), sem("w_hi_by_dve"), sem("w_ready")
        E_hi_done = sem("E_hi_done")
        filled = [sem(f"filled{i}") for i in range(8)]
        emptied = [sem(f"emptied{i}") for i in range(8)]
        xT_hi, qk_hi, sT_hi, s2T_hi = sem("xT_hi"), sem("qk_hi"), sem("sT_hi"), sem("s2T_hi")
        nmax_ready = sem("nmax_ready")
        var_ready = [sem("var1_ready"), sem("var2_ready")]
        rstd_ready = [sem("rstd1_ready"), sem("rstd2_ready")]
        norm_ready = [sem("norm1_ready"), sem("norm2_ready")]
        q_filled, qhi_done, qlo_done = sem("q_filled"), sem("qhi_done"), sem("qlo_done")
        diag_filled, off_filled = sem("diag_filled"), sem("off_filled")
        diag_done, off_done, masked = sem("diag_done"), sem("off_done"), sem("masked")
        r_done, rts_done = sem("r_done"), sem("rts_done")
        lg_ready, gexp_done, disp_ready = sem("lg_ready"), sem("gexp_done"), sem("disp_ready")
        d_stored = sem("d_stored")
        dbc_ld = [[sem(f"dbc_ld{h}_{c}") for c in range(len(CHUNKS) - 1)] for h in range(HALVES)]
        u1_filled, u2_filled, sil_done, uu_done, hid_done, hid_by_dve, down_done = (
            sem(n) for n in ("u1_filled", "u2_filled", "sil_done", "uu_done", "hid_done", "hid_by_dve", "down_done"))
        yts_done, y_filled, res_ready, stored = sem("yts_done"), sem("y_filled"), sem("res_ready"), sem("stored")
        dve_step, pool_step = sem("dve_step"), sem("pool_step")

        def bank_of(use, i):
            return banks[turns[use, i][0]]

        def wait_free(eng, use, i):
            bank, nth = turns[use, i]
            if nth > 1:
                eng.wait_ge(emptied[bank], nth - 1)

        def wait_filled(eng, use, i):
            bank, nth = turns[use, i]
            eng.wait_ge(filled[bank], nth)

        def wait_emptied(eng, use, i):
            bank, nth = turns[use, i]
            eng.wait_ge(emptied[bank], nth)

        def is_filled(use, i):
            return filled[turns[use, i][0]]

        def is_emptied(use, i):
            return emptied[turns[use, i][0]]

        def wait_hid(eng, unit, piece=0):
            before = sum(on_dve(n) for n in range(unit + 1))
            if on_dve(unit):
                eng.wait_ge(hid_by_dve, before + piece)
            else:
                eng.wait_ge(hid_done, unit + 1 - before)

        def img(b):
            return slice(b * TOKENS, (b + 1) * TOKENS)

        def tile(t):
            return slice(t * P, (t + 1) * P)

        block = ctx.enter_context(nc.Block())

        @block.sync
        def _(sp):
            def load_halves(dst, src, s):
                for half in range(2):
                    sp.dma_start(dst[C * half:C * (half + 1)], src).then_inc(s, 16)

            sp.dma_start(x_in[:, 0:TILES, :], x_tok[:, 0:TILES, :]).then_inc(ld_x0, 16)
            for m, w in enumerate((wq, wk)):
                sp.dma_start(wqk_in[:, m, :], w.unsqueeze(0).to_broadcast([2, C, QK])).then_inc(ld_wqk, 16)
            for m, b in enumerate((bq, bk)):
                sp.dma_start(b_in[0:1, m, :], b.unsqueeze(0)).then_inc(ld_b, 16)
            sp.dma_start(wv_in[:], wv.unsqueeze(0).to_broadcast([2, C, C])).then_inc(ld_wv, 16)
            sp.dma_start(x_in[:, TILES:NT, :], x_tok[:, TILES:NT, :]).then_inc(ld_x, 16)
            sp.dma_start(q_in[:], Q.rearrange("h i j -> i h j")).then_inc(ld_q, 16)
            sp.dma_start(e_in[:], E.rearrange("(m g) i k -> (g i) m k", g=2)).then_inc(ld_e, 16)
            for m, w in enumerate((w1, w2)):
                load_halves(w_in[:, m, :].rearrange("p (e h) -> p e h", e=EXPERTS), w.rearrange("e c h -> c e h"), ld_w)
            sp.dma_start(gate_in[:], gate_w.unsqueeze(0).to_broadcast([2, C, EXPERTS])).then_inc(ld_gate, 16)
            sp.dma_start(w3_in[:], w3.rearrange("e h c -> h e c")).then_inc(ld_w3, 16)
            for name, i in SCHEDULE:
                if name == "spread weights":
                    wait_emptied(sp, "dT", i)
                    sp.dma_start(d_scratch[i].rearrange("e (t p) -> t e p", p=P), dispT[:, i, :]).then_inc(d_stored, 16)
                    sp.wait_ge(d_stored, 16 * (i + 1))
                    for c in range(len(CHUNKS) - 1):
                        experts = slice(CHUNKS[c], CHUNKS[c + 1])
                        if i == 1:
                            wait_hid(sp, experts.stop - 2)
                            wait_hid(sp, experts.stop - 1)
                        src = d_scratch[i, experts, :].rearrange("e t -> (e t)").unsqueeze(0)
                        sp.dma_start(dbc[:, experts, :].rearrange("p e t -> p (e t)"),
                                     src.to_broadcast([P, (experts.stop - experts.start) * HALF])).then_inc(dbc_ld[i][c], 16)
                if name == "output" or (name, i) == ("last experts", 1):
                    half = 0 if name == "output" else 1
                    for k in range(0, HTILES, 2):
                        sp.wait_ge(res_ready, HTILES // 2 * half + k // 2 + 1)
                        t = HTILES * half + k
                        sp.dma_start(out_tok[:, t:t + 2, :], x2[:, t:t + 2, :]).then_inc(stored, 16)
            sp.wait_ge(stored, 16 * HALVES * HTILES // 2)

        @block.gpsimd
        def _(pool):
            def wait_step(ins, count=[0]):
                count[0] += 1
                ins.then_inc(pool_step, 1)
                pool.wait_ge(pool_step, count[0])

            pool.memset(ident[:], 0.0).then_inc(zeroed, 1)
            pool.memset(b_row[:], 0.0).then_inc(zeroed, 1)
            for part in wqk:
                pool.memset(part[:].bitcast(FP32), 0.0).then_inc(zeroed, 1)
            pool.wait_ge(zeroed, 4)
            pool.affine_select(out=ident[:], in_=ident[:], compare_op=ALU.not_equal, fill=1.0, base=0,
                               pattern=[[-1, P]], channel_multiplier=1).then_inc(consts, 1)
            pool.dma_start(gamma_in[:], gamma.unsqueeze(0).to_broadcast([P, 1])).then_inc(ld_bv, 16)
            pool.dma_start(bv_in[:], bv.unsqueeze(0).to_broadcast([P, C])).then_inc(ld_bv, 16)
            pool.memset(v[:, :, :, C:C + 1], 1.0).then_inc(consts, 1)
            pool.memset(neg_half[:], -0.5)
            wait_step(pool.memset(twin[:], 0.0))
            wait_step(pool.affine_select(out=twin[:], in_=twin[:], compare_op=ALU.not_equal, fill=1.0, base=0,
                                         pattern=[[-1, C]], channel_multiplier=1))
            pool.affine_select(out=twin[:], in_=twin[:], compare_op=ALU.not_equal, fill=1.0, base=-C,
                               pattern=[[-1, C]], channel_multiplier=1).then_inc(consts, 1)
            pool.dma_start(gate_b_in[:], gate_b.unsqueeze(0).to_broadcast([P, EXPERTS])).then_inc(ld_gate_b, 16)
            pool.wait_ge(ld_bv, 32)
            pool.wait_ge(ld_wv, 16)
            wait_step(nc.gpsimd.tensor_scalar(wv_gamma[:], wv_in[:], gamma_in[:, 0:1], None, ALU.mult))
            wait_step(nc.gpsimd.tensor_scalar(bv_gamma[:], bv_in[:], gamma_in[:, 0:1], None, ALU.mult))
            wait_step(nc.gpsimd.tensor_copy(wvs[:, 0], wv_gamma[:]))
            nc.gpsimd.tensor_tensor(wvs[:, 1], wv_gamma[:], wvs[:, 0].bitcast(FP32), ALU.subtract).then_inc(wv_ready, 1)

            for name, i in SCHEDULE:
                if name in ("residual 1", "residual 2"):
                    norm = 0 if name == "residual 1" else 1
                    pool.wait_ge(var_ready[norm], i + 1)
                    nc.gpsimd.tensor_tensor(rstd[:, norm, i, :], veps[:, norm, i, :], neg_half[:],
                                            ALU.pow).then_inc(rstd_ready[norm], 1)
                if name == "split gate":
                    pool.wait_ge(ld_gate, 16)
                    wait_step(nc.gpsimd.tensor_copy(gates[:, 0], gate_in[:]))
                    nc.gpsimd.tensor_tensor(gates[:, 1], gate_in[:], gates[:, 0].bitcast(FP32),
                                            ALU.subtract).then_inc(gate_ready, 1)
                if name == "split w":
                    pool.wait_ge(w_hi_done if i % 2 == 0 else w_hi_by_dve, i // 2 + 1)
                    cols = slice(2 * i * HIDDEN, 2 * (i + 1) * HIDDEN)
                    nc.gpsimd.tensor_tensor(ws[1][:, :, cols], w_in[:, :, cols], ws[0][:, :, cols].bitcast(FP32),
                                            ALU.subtract).then_inc(w_ready, 1)
                if name == "mask":
                    pool.wait_ge(diag_done, i + 1)
                    blocks = omega[:, i % OM, 0:2].rearrange("p d h t -> p (d h) t")
                    pool.affine_select(out=blocks, in_=blocks, compare_op=ALU.is_ge, fill=0.0, base=0,
                                       pattern=[[0, 4], [1, P]], channel_multiplier=-1).then_inc(masked, 1)
                if name == "expert" and not on_dve(i):
                    half, e = divmod(i, EXPERTS)
                    pool.wait_ge(uu_done, i + 1)
                    if e in CHUNKS:
                        pool.wait_ge(dbc_ld[half][chunk_of(e)], 16)
                    if i >= HID:
                        pool.wait_ge(down_done, (i - HID) // 2 + 1)
                    nc.gpsimd.tensor_tensor(hid[:, i % HID], uu[:, i % UU], dbc[:, e, :],
                                            ALU.mult).then_inc(hid_done, 1)

        @block.scalar
        def _(act):
            def hi_part_of(stack, use, b, s, rows=C):
                wait_filled(act, use, b)
                nc.scalar.activation(stack[0:rows, img(b)], bank_of(use, b)[0:rows, 0:TOKENS], ACT.Copy).then_inc(s, 1)

            for name, i in SCHEDULE:
                if name == "stack x":
                    hi_part_of(xT, "xT", i, xT_hi)
                if name == "stack s":
                    hi_part_of(s_parts[0], "sT", i, sT_hi, rows=P)
                if name == "stack s2":
                    hi_part_of(s2T, "s2T", i, s2T_hi)
                if name == "split e":
                    wait_filled(act, "eT", 0)
                    nc.scalar.activation(Es[0:C, :], bank_of("eT", 0)[0:C, :], ACT.Copy).then_inc(E_hi_done, 1)
                if name == "split q":
                    act.wait_ge(ld_q, 16)
                    heads = slice(4 * i, 4 * (i + 1))
                    nc.scalar.activation(Qs[0:C, heads], q_in[:, heads], ACT.Copy).then_inc(Q_hi_done, 1)
                if name == "split w" and i % 2 == 0:
                    act.wait_ge(ld_w, 64)
                    cols = slice(2 * i * HIDDEN, 2 * (i + 1) * HIDDEN)
                    nc.scalar.activation(ws[0][:, :, cols], w_in[:, :, cols], ACT.Copy).then_inc(w_hi_done, 1)
                if name == "copy qk":
                    for m, use in enumerate("qk"):
                        if i == 0 and m == 0:
                            wait_emptied(act, "bias", 0)
                        wait_filled(act, use, i)
                        if i >= 2:
                            wait_emptied(act, use, i - 2)
                        nc.scalar.activation(hi_part[:, i % 2, m, :], bank_of(use, i)[:, 0:TOKENS], ACT.Identity,
                                             bias=b_col[:, 2 + m:3 + m], scale=lo_rows[:, m:m + 1]).then_inc(qk_hi, 1)
                if name == "exp":
                    act.wait_ge(nmax_ready, i + 1)
                    for k in range(TILES):
                        last = nc.scalar.activation(prob[:, i % 2, k, :], bank_of("S", i)[:, k * TOKENS:(k + 1) * TOKENS],
                                                    ACT.Exp, bias=nmax[:, i % 2, k:k + 1])
                    last.then_inc(is_emptied("S", i), 1)
                if name == "copy prob":
                    wait_filled(act, "PT", i)
                    if i >= 2:
                        wait_filled(act, "PV", i - 2)
                    nc.scalar.activation(probT[:, i % 2].rearrange("p j n -> p (j n)"), bank_of("PT", i)[:],
                                         ACT.Copy).then_inc(is_emptied("PT", i), 1)
                if name == "copy es":
                    if i >= 2:
                        act.wait_ge(r_done, PAIRS * (i - 1))
                    wait_filled(act, "es0", i)
                    nc.scalar.activation(es[:, i % 2, 0, :], bank_of("es0", i)[:],
                                         ACT.Copy).then_inc(is_emptied("es0", i), 1)
                if name == "copy query":
                    act.wait_ge(q_filled, i + 1)
                    if i >= QS:
                        act.wait_ge(off_filled, i - QS + 1)
                    for hh, rows in enumerate((slice(0, C), slice(C, P))):
                        nc.scalar.activation(q_stack[rows, i % QS, hh, :], banks[Q_BANK[i % 2]][rows, 0:TOKENS],
                                             ACT.Copy).then_inc(qhi_done, 1)
                if name == "mask":
                    act.wait_ge(diag_filled, i + 1)
                    if i >= OM:
                        act.wait_ge(r_done, i - OM + 1)
                    nc.scalar.activation(omega[:, i % OM, 0:2].rearrange("p d h t -> p (d h t)"),
                                         banks[DIAG_BANK[i % 2]][:], ACT.Copy).then_inc(diag_done, 1)
                    act.wait_ge(off_filled, i + 1)
                    nc.scalar.activation(omega[:, i % OM, 2].rearrange("p h t -> p (h t)"),
                                         banks[OFF_BANK][:, 0:2 * P], ACT.Copy).then_inc(off_done, 1)
                if name == "copy sum":
                    act.wait_ge(r_done, PAIRS * (i + 1))
                    if i >= 2:
                        wait_filled(act, "r", i - 2)
                    nc.scalar.activation(rts[:, i % 2, :], banks[RT_BANK][:, 0:TOKENS], ACT.Copy).then_inc(rts_done, 1)
                if name == "gate exp":
                    act.wait_ge(lg_ready, i + 1)
                    nc.scalar.activation(gp[:], lg[:], ACT.Exp).then_inc(gexp_done, 1)
                if name == "spread weights":
                    wait_filled(act, "dT", i)
                    nc.scalar.activation(dispT[:, i, :], bank_of("dT", i)[0:HTILES * EXPERTS, 0:P],
                                         ACT.Copy).then_inc(is_emptied("dT", i), 1)
                if name == "expert":
                    act.wait_ge(u1_filled, i + 1)
                    if i >= SIL and on_dve(i - SIL):
                        wait_hid(act, i - SIL)
                    elif i >= SIL:
                        act.wait_ge(uu_done, i - SIL + 1)
                    nc.scalar.activation(sil[:, i % SIL], banks[U1_BANK[i % 2]][:], ACT.Silu).then_inc(sil_done, 1)
                if name in ("output", "gather"):
                    half = 0 if name == "output" else 1
                    act.wait_ge(down_done, EXPERTS // 2 if half == 0 else UNITS // 2 - 1)
                    for cols in (slice(0, HALF // 2), slice(HALF // 2, HALF)):
                        nc.scalar.activation(yts[:, half, cols], banks[Y_BANK[half]][:, cols], ACT.Copy).then_inc(yts_done, 1)

        @block.vector
        def _(dve):
            def wait_step(ins, count=[0]):
                count[0] += 1
                ins.then_inc(dve_step, 1)
                dve.wait_ge(dve_step, count[0])

            def lo_part_of(stack, use, b, hi_sem):
                dve.wait_ge(hi_sem, b + 1)
                nc.vector.tensor_tensor(stack[C:P, img(b)], bank_of(use, b)[0:C, 0:TOKENS],
                                        stack[0:C, img(b)].bitcast(FP32), ALU.subtract).then_inc(is_emptied(use, b), 1)

            def statistics(norm, b, src):
                for k in range(TILES):
                    last = nc.vector.bn_stats(stats[:, norm, k, :], src[:, TILES * b + k, :])
                wait_step(last)
                for k in range(TILES):
                    last = nc.vector.bn_aggr(mv[:, norm, b, k, :], stats[:, norm, k, :])
                wait_step(last)
                nc.vector.tensor_scalar(veps[:, norm, b, :], mv[:, norm, b, :, 1], EPS, None,
                                        ALU.add).then_inc(var_ready[norm], 1)

            def normalise(norm, b, src):
                dve.wait_ge(rstd_ready[norm], b + 1)
                for k in range(TILES):
                    tokens = src[:, TILES * b + k, :]
                    last = nc.vector.tensor_scalar(
                        sd[:, b % 2, k] if norm == 0 else s2[:, b % 2, k],
                        tokens.unsqueeze(1).to_broadcast([P, 2, C]) if norm == 0 else tokens,
                        mv[:, norm, b, k, 0:1], rstd[:, norm, b, k:k + 1], ALU.subtract, ALU.mult)
                last.then_inc(norm_ready[norm], 1)

            wait_step(nc.vector.memset(lo_rows[:], 0.0))
            for rows, m in ((slice(32, 64), 0), (slice(96, 128), 0), (slice(64, 128), 1)):
                wait_step(nc.vector.memset(lo_rows[rows, m:m + 1], 1.0))
            dve.wait_ge(zeroed, 4)

            for name, i in SCHEDULE:
                if name == "project qk" and i == 0:
                    dve.wait_ge(ld_wqk, 32)
                    four = [wqk_in[:, m, :].unsqueeze(1).to_broadcast([P, 4, QK]) for m in range(2)]
                    for m in range(2):
                        last = nc.vector.tensor_copy(wqk[0][:, m, :, 0:QK], four[m])
                    wait_step(last)
                    for m in range(2):
                        last = nc.vector.tensor_tensor(wqk[1][:, m, :, 0:QK], four[m],
                                                       wqk[0][:, m, :, 0:QK].bitcast(FP32), ALU.subtract)
                    last.then_inc(wqk_ready, 1)
                if name == "bias":
                    dve.wait_ge(ld_b, 32)
                    nc.vector.tensor_copy(b_row[0:1, :, :, 0:QK],
                                          b_in[0:1].unsqueeze(2).to_broadcast([1, 2, 4, QK])).then_inc(b_row_ready, 1)
                    wait_filled(dve, "bias", 0)
                    wait_step(nc.vector.tensor_copy(b_col[:, 0:2], bank_of("bias", 0)[:, 0:2]))
                    nc.vector.tensor_tensor(b_col[:, 2:4], b_col[:, 0:2], lo_rows[:],
                                            ALU.mult).then_inc(is_emptied("bias", 0), 1)
                if name == "stack x":
                    lo_part_of(xT, "xT", i, xT_hi)
                if name == "stack s":
                    dve.wait_ge(sT_hi, i + 1)
                    nc.vector.tensor_tensor(s_parts[1][:, img(i)], bank_of("sT", i)[:, 0:TOKENS],
                                            s_parts[0][:, img(i)].bitcast(FP32), ALU.subtract).then_inc(is_emptied("sT", i), 1)
                if name == "stack s2":
                    lo_part_of(s2T, "s2T", i, s2T_hi)
                if name == "split e":
                    dve.wait_ge(E_hi_done, 1)
                    nc.vector.tensor_tensor(Es[C:P, :], bank_of("eT", 0)[0:C, :], Es[0:C, :].bitcast(FP32),
                                            ALU.subtract).then_inc(is_emptied("eT", 0), 1)
                if name == "split q":
                    dve.wait_ge(Q_hi_done, i + 1)
                    heads = slice(4 * i, 4 * (i + 1))
                    nc.vector.tensor_tensor(Qs[C:P, heads], q_in[:, heads], Qs[0:C, heads].bitcast(FP32),
                                            ALU.subtract).then_inc(Q_ready, 1)
                if name == "copy qk":
                    for m, use in enumerate("qk"):
                        if i == 0 and m == 0:
                            wait_emptied(dve, "bias", 0)
                        dve.wait_ge(qk_hi, 2 * i + m + 1)
                        nc.vector.scalar_tensor_tensor(out=qk[:, i % 2, m, :], in0=bank_of(use, i)[:, 0:TOKENS],
                                                       scalar=b_col[:, m:m + 1], in1=hi_part[:, i % 2, m, :].bitcast(FP32),
                                                       op0=ALU.add, op1=ALU.subtract).then_inc(is_emptied(use, i), 1)
                if name == "copy v":
                    wait_filled(dve, "v", i)
                    if i == 0:
                        dve.wait_ge(consts, 2)
                        dve.wait_ge(wv_ready, 1)
                    products = bank_of("v", i)[:, 0:TILES * 2 * C].rearrange("p (k s c) -> p k s c", k=TILES, s=2)
                    wait_step(nc.vector.tensor_tensor(v_part[:, i], products[:, :, 1],
                                                      bv_gamma[:].unsqueeze(1).to_broadcast([P, TILES, C]), ALU.add))
                    nc.vector.tensor_tensor(v[:, i, :, 0:C], products[:, :, 0], v_part[:, i],
                                            ALU.add).then_inc(is_emptied("v", i), 1)
                if name == "exp":
                    wait_filled(dve, "S", i)
                    nc.vector.tensor_reduce(nmax[:, i % 2, :],
                                            bank_of("S", i)[:].rearrange("p (k m) -> p k m", k=TILES), AX.X, ALU.max,
                                            negate=True).then_inc(nmax_ready, 1)
                if name == "residual 1":
                    wait_filled(dve, "PV", i)
                    pv = bank_of("PV", i)[:, 0:TILES * (C + 1)].rearrange("p (k c) -> p k c", k=TILES)
                    wait_step(nc.vector.reciprocal(rsum[:, i % 2, :], pv[:, :, C]))
                    for k in range(TILES):
                        last = nc.vector.scalar_tensor_tensor(
                            out=x1[:, TILES * i + k, :], in0=pv[:, k, 0:C], scalar=rsum[:, i % 2, k:k + 1],
                            in1=x_in[:, TILES * i + k, :], op0=ALU.mult, op1=ALU.add)
                    last.then_inc(is_emptied("PV", i), 1)
                    wait_emptied(dve, "PV", i)
                    statistics(0, i, x1)
                if name == "normalise 1":
                    normalise(0, i, x1)
                if name == "split w" and i % 2 == 1:
                    dve.wait_ge(ld_w, 64)
                    cols = slice(2 * i * HIDDEN, 2 * (i + 1) * HIDDEN)
                    nc.vector.tensor_copy(ws[0][:, :, cols], w_in[:, :, cols]).then_inc(w_hi_by_dve, 1)
                if name == "copy es":
                    if i >= 2:
                        dve.wait_ge(r_done, PAIRS * (i - 1))
                    wait_filled(dve, "es1", i)
                    nc.vector.tensor_copy(es[:, i % 2, 1, :], bank_of("es1", i)[:]).then_inc(is_emptied("es1", i), 1)
                if name == "copy query":
                    for hh, (rows, other) in enumerate(((slice(0, C), slice(C, P)), (slice(C, P), slice(0, C)))):
                        dve.wait_ge(qhi_done, 2 * i + hh + 1)
                        last = nc.vector.tensor_tensor(q_stack[other, i % QS, hh, :], banks[Q_BANK[i % 2]][rows, 0:TOKENS],
                                                       q_stack[rows, i % QS, hh, :].bitcast(FP32), ALU.subtract)
                    last.then_inc(qlo_done, 1)
                if name == "residual 2":
                    wait_filled(dve, "r", i)
                    tiles = slice(TILES * i, TILES * (i + 1))
                    sums = bank_of("r", i)[:, 0:TILES * P].rearrange("p (k s c) -> p k s c", k=TILES, s=2)
                    wait_step(nc.vector.tensor_tensor(x2[:, tiles, :], x1[:, tiles, :], sums[:, :, 0], ALU.add))
                    nc.vector.tensor_tensor(x2[:, tiles, :], x2[:, tiles, :], sums[:, :, 1],
                                            ALU.add).then_inc(is_emptied("r", i), 1)
                    wait_emptied(dve, "r", i)
                    statistics(1, i, x2)
                if name == "normalise 2":
                    normalise(1, i, x2)
                spread = [P, HTILES, EXPERTS]
                if name == "gate exp":
                    wait_filled(dve, "lg", i)
                    if i == 0:
                        dve.wait_ge(ld_gate_b, 16)
                    products = bank_of("lg", i)[:, 0:HTILES * 2 * EXPERTS].rearrange("p (t s e) -> p t s e", t=HTILES, s=2)
                    wait_step(nc.vector.tensor_tensor(lg_part[:, i], products[:, :, 1],
                                                      gate_b_in[:].unsqueeze(1).to_broadcast(spread), ALU.add))
                    nc.vector.tensor_tensor(lg[:], products[:, :, 0], lg_part[:, i], ALU.add).then_inc(is_emptied("lg", i), 1)
                    wait_emptied(dve, "lg", i)
                    wait_step(nc.vector.tensor_reduce(lmax[:], lg[:], AX.X, ALU.max))
                    nc.vector.tensor_tensor(lg[:], lg[:], lmax[:].unsqueeze(2).to_broadcast(spread),
                                            ALU.subtract).then_inc(lg_ready, 1)
                if name == "gate top":
                    dve.wait_ge(gexp_done, i + 1)
                    wait_step(nc.vector.tensor_reduce(gsum[:], gp[:], AX.X, ALU.add))
                    wait_step(nc.vector.reciprocal(grec[:], gsum[:]))
                    wait_step(nc.vector.tensor_tensor(probs[:], gp[:], grec[:].unsqueeze(2).to_broadcast(spread), ALU.mult))
                    for t in range(HTILES):
                        last = nc.vector.max(top8[:, t, :], probs[:, t, :])
                    wait_step(last)
                    wait_step(nc.vector.tensor_tensor(tsum[:], top8[:, :, 0], top8[:, :, 1], ALU.add))
                if name == "gate weights":
                    nc.vector.reciprocal(trec[:], tsum[:])
                    wait_step(nc.vector.memset(top8[:, :, 2:8], -1.0))
                    for t in range(HTILES):
                        last = nc.vector.match_replace(out=rest[:, t, :], in_to_replace=top8[:, t, :],
                                                       in_values=probs[:, t, :], imm_value=0.0)
                    wait_step(last)
                    wait_step(nc.vector.tensor_tensor(dsel[:], probs[:], rest[:], ALU.subtract))
                    nc.vector.tensor_tensor(disp[:], dsel[:], trec[:].unsqueeze(2).to_broadcast(spread),
                                            ALU.mult).then_inc(disp_ready, 1)
                if name == "expert":
                    dve.wait_ge(u2_filled, i + 1)
                    if i >= UU and not on_dve(i - UU):
                        wait_hid(dve, i - UU)
                    if not on_dve(i):
                        dve.wait_ge(sil_done, i + 1)
                        nc.vector.tensor_tensor(uu[:, i % UU], banks[U2_BANK[i % 2]][:], sil[:, i % SIL],
                                                ALU.mult).then_inc(uu_done, 1)
                    else:
                        half, e = divmod(i, EXPERTS)
                        dve.wait_ge(dbc_ld[half][chunk_of(e)], 16)
                        nc.vector.tensor_tensor(uu[:, i % UU], banks[U2_BANK[i % 2]][:], dbc[:, e, :],
                                                ALU.mult).then_inc(uu_done, 1)
                        dve.wait_ge(uu_done, i + 1)
                        dve.wait_ge(sil_done, i + 1)
                        if i >= HID:
                            dve.wait_ge(down_done, (i - HID) // 2 + 1)
                        pieces = (slice(0, HALF),) if i < UNITS - 1 else (slice(0, HALF // 2), slice(HALF // 2, HALF))
                        for cols in pieces:
                            nc.vector.tensor_tensor(hid[:, i % HID, cols], uu[:, i % UU, cols], sil[:, i % SIL, cols],
                                                    ALU.mult).then_inc(hid_by_dve, 1)
                if name == "output" or (name, i) == ("last experts", 1):
                    half = 0 if name == "output" else 1
                    for k in range(0, HTILES, 2):
                        t = HTILES * half + k
                        dve.wait_ge(y_filled, HTILES // 2 * half + k // 2 + 1)
                        if half == 0:
                            sums = banks[SHARED_BANKS[k // 2]][:, 0:2 * P].rearrange("p (t s c) -> p t s c", t=2, s=2)
                            wait_step(nc.vector.tensor_tensor(x2[:, t:t + 2, :], x2[:, t:t + 2, :], sums[:, :, 0], ALU.add))
                            nc.vector.tensor_tensor(x2[:, t:t + 2, :], x2[:, t:t + 2, :], sums[:, :, 1],
                                                    ALU.add).then_inc(res_ready, 1)
                            continue
                        nc.vector.tensor_tensor(x2[:, t:t + 2, :], x2[:, t:t + 2, :],
                                                banks[SHARED_BANKS[k // 2]][:, 0:2 * C].rearrange("p (t c) -> p t c", t=2),
                                                ALU.add).then_inc(res_ready, 1)

        @block.tensor
        def _(pe):
            def two_pass(dst, weights, moving):
                nc.tensor.matmul(dst, weights[0], moving[0], start=True, stop=False)
                return nc.tensor.matmul(dst, weights[1], moving[1], start=False, stop=True)

            def transpose_tiles(use, b, tiles):
                wait_free(pe, use, b)
                for k, src in enumerate(tiles):
                    last = nc.tensor.transpose(bank_of(use, b)[0:src.shape[-1], tile(k)], src, ident[:])
                last.then_inc(is_filled(use, b), 1)

            for name, i in SCHEDULE:
                if name == "bias":
                    pe.wait_ge(consts, 1)
                    pe.wait_ge(b_row_ready, 1)
                    for m in range(2):
                        last = nc.tensor.transpose(bank_of("bias", 0)[:, m:m + 1], b_row[0:1, m].rearrange("o g n -> o (g n)"),
                                                   ident[0:1, 0:1])
                    last.then_inc(is_filled("bias", 0), 1)
                if name == "transpose x":
                    if i == 0:
                        pe.wait_ge(consts, 1)
                    pe.wait_ge(ld_x0 if i == 0 else ld_x, 16)
                    transpose_tiles("xT", i, [x_in[:, TILES * i + k] for k in range(TILES)])
                if name == "transpose e":
                    pe.wait_ge(ld_e, 16)
                    transpose_tiles("eT", i, [e_in[:, m] for m in range(PAIRS)])
                if name == "project qk":
                    if i == 0:
                        pe.wait_ge(wqk_ready, 1)
                    wait_emptied(pe, "xT", i)
                    for m, use in enumerate("qk"):
                        wait_free(pe, use, i)
                        two_pass(bank_of(use, i)[:, 0:TOKENS], [part[:, m].rearrange("p g n -> p (g n)") for part in wqk],
                                 [xT[:, img(i)]] * 2).then_inc(is_filled(use, i), 1)
                if name == "project v":
                    if i == 0:
                        pe.wait_ge(wv_ready, 1)
                    wait_emptied(pe, "xT", i)
                    wait_free(pe, "v", i)
                    for k in range(TILES):
                        last = nc.tensor.matmul(bank_of("v", i)[:, 2 * C * k:2 * C * (k + 1)], xT[:, tile(TILES * i + k)],
                                                wvs[:].rearrange("p s c -> p (s c)"), start=True, stop=True)
                    last.then_inc(is_filled("v", i), 1)
                if name == "score":
                    wait_emptied(pe, "q", i)
                    wait_emptied(pe, "k", i)
                    wait_free(pe, "S", i)
                    for k in range(TILES):
                        last = nc.tensor.matmul(bank_of("S", i)[:, k * TOKENS:(k + 1) * TOKENS], qk[:, i % 2, 0, tile(k)],
                                                qk[:, i % 2, 1, :], start=True, stop=True)
                    last.then_inc(is_filled("S", i), 1)
                if name == "transpose prob":
                    wait_emptied(pe, "S", i)
                    transpose_tiles("PT", i, [prob[:, i % 2, k, tile(j)] for j in range(TILES) for k in range(TILES)])
                if name == "attend":
                    wait_emptied(pe, "PT", i)
                    wait_emptied(pe, "v", i)
                    wait_free(pe, "PV", i)
                    for k in range(TILES):
                        for j in range(TILES):
                            last = nc.tensor.matmul(bank_of("PV", i)[:, (C + 1) * k:(C + 1) * (k + 1)],
                                                    probT[:, i % 2, j, tile(k)], v[:, i, j, :],
                                                    start=(j == 0), stop=(j == TILES - 1))
                    last.then_inc(is_filled("PV", i), 1)
                if name == "transpose s":
                    pe.wait_ge(norm_ready[0], i + 1)
                    transpose_tiles("sT", i, [sd[:, i % 2, k].rearrange("p d c -> p (d c)") for k in range(TILES)])
                if name == "project es":
                    if i == 0:
                        wait_emptied(pe, "eT", 0)
                    wait_emptied(pe, "sT", i)
                    for u in range(TILES):
                        use = f"es{u}"
                        wait_free(pe, use, i)
                        two_pass(bank_of(use, i)[:], [part[:, tile(TILES * i + u)] for part in s_parts],
                                 [Es[:]] * 2).then_inc(is_filled(use, i), 1)
                b, pair = divmod(i, PAIRS)
                if name == "query":
                    if i == 0:
                        for bank in (*Q_BANK, *DIAG_BANK, OFF_BANK, RT_BANK):
                            pe.wait_ge(emptied[bank], early_uses[bank])
                    if pair == 0:
                        wait_emptied(pe, "sT", b)
                    if b == 0:
                        pe.wait_ge(Q_ready, 1 + pair // 2)
                    if i >= 2:
                        pe.wait_ge(qlo_done, i - 1)
                    two_pass(banks[Q_BANK[i % 2]][:, 0:TOKENS],
                             [Qs[:, 2 * pair:2 * pair + 2].rearrange("p h j -> p (h j)")] * 2,
                             [part[:, img(b)] for part in s_parts]).then_inc(q_filled, 1)
                if name == "causal":
                    pe.wait_ge(qlo_done, i + 1)
                    u = [[part[:, tile(TILES * b + k)] for part in s_parts] for k in range(TILES)]
                    at = [[q_stack[:, i % QS, :, tile(k)]] * 2 for k in range(TILES)]
                    if i >= 2:
                        pe.wait_ge(diag_done, i - 1)
                    two_pass(banks[DIAG_BANK[i % 2]][:, 0:2 * P], u[0], at[0])
                    two_pass(banks[DIAG_BANK[i % 2]][:, 2 * P:4 * P], u[1], at[1]).then_inc(diag_filled, 1)
                    if i >= 1:
                        pe.wait_ge(off_done, i)
                    two_pass(banks[OFF_BANK][:, 0:2 * P], u[0], at[1]).then_inc(off_filled, 1)
                if name == "sum":
                    pe.wait_ge(off_done, i + 1)
                    pe.wait_ge(masked, i + 1)
                    if pair == 0:
                        wait_emptied(pe, "es0", b)
                        wait_emptied(pe, "es1", b)
                        if b >= 1:
                            pe.wait_ge(rts_done, b)
                    for u in range(2):
                        for hh in range(2):
                            h = 2 * pair + hh
                            blocks = omega[:, i % OM, 0:3:2, hh, :] if u == 0 else omega[:, i % OM, 1, hh, :]
                            last = nc.tensor.matmul(banks[RT_BANK][C * hh:C * (hh + 1), P * u:TOKENS],
                                                    es[:, b % 2, u, C * h:C * (h + 1)], blocks,
                                                    start=(pair == 0 and u == 0), stop=(pair == PAIRS - 1 and u == 1))
                    last.then_inc(r_done, 1)
                if name == "untranspose sum":
                    pe.wait_ge(rts_done, i + 1)
                    transpose_tiles("r", i, [rts[:, i % 2, tile(k)] for k in range(TILES)])
                if name == "transpose s2":
                    pe.wait_ge(norm_ready[1], i + 1)
                    transpose_tiles("s2T", i, [s2[:, i % 2, k] for k in range(TILES)])
                if name == "gate":
                    if i == 0:
                        pe.wait_ge(gate_ready, 1)
                    wait_emptied(pe, "s2T", 2 * i)
                    wait_emptied(pe, "s2T", 2 * i + 1)
                    wait_free(pe, "lg", i)
                    for t in range(HTILES):
                        last = nc.tensor.matmul(bank_of("lg", i)[:, 2 * EXPERTS * t:2 * EXPERTS * (t + 1)],
                                                s2T[:, tile(HTILES * i + t)], gates[:].rearrange("p s e -> p (s e)"),
                                                start=True, stop=True)
                    last.then_inc(is_filled("lg", i), 1)
                if name == "transpose weights":
                    pe.wait_ge(disp_ready, i + 1)
                    wait_free(pe, "dT", i)
                    nc.tensor.transpose(bank_of("dT", i)[0:HTILES * EXPERTS, 0:P], disp[:].rearrange("p t e -> p (t e)"),
                                        ident[:]).then_inc(is_filled("dT", i), 1)
                if name == "up":
                    half, e = divmod(i, EXPERTS)
                    if e == 0:
                        wait_emptied(pe, "s2T", 2 * half)
                        wait_emptied(pe, "s2T", 2 * half + 1)
                    if i < EXPERTS and e % 2 == 0:
                        pe.wait_ge(w_ready, e // 2 + 1)
                    if i < 2:
                        pe.wait_ge(qlo_done, IMAGES * PAIRS - 1 + i)
                        pe.wait_ge(diag_done, IMAGES * PAIRS - 1 + i)
                    else:
                        pe.wait_ge(uu_done, i - 1)
                        if on_dve(i - 2):
                            pe.wait_ge(sil_done, i - 1)
                    moving = s2T[:, half * HALF:(half + 1) * HALF]
                    products = [(0, U1_BANK, u1_filled), (1, U2_BANK, u2_filled)]
                    for m, bank, full in products if i < UNITS - 1 else products[::-1]:
                        two_pass(banks[bank[i % 2]][:], [part[:, m, HIDDEN * e:HIDDEN * (e + 1)] for part in ws],
                                 [moving] * 2).then_inc(full, 1)
                if name == "down":
                    half, e = divmod(2 * i, EXPERTS)
                    if i == 0:
                        pe.wait_ge(ld_w3, 16)
                        pe.wait_ge(off_done, IMAGES * PAIRS)
                    if i == EXPERTS // 2:
                        pe.wait_ge(rts_done, IMAGES)
                    wait_hid(pe, 2 * i)
                    wait_hid(pe, 2 * i + 1)
                    last_pair = EXPERTS - 2 if half == 0 else EXPERTS - 4
                    for n in range(2):
                        last = nc.tensor.matmul(banks[Y_BANK[half]][C * n:C * (n + 1), :], w3_in[:, e + n, :],
                                                hid[:, (2 * i + n) % HID], start=(e == 0), stop=(e == last_pair))
                    last.then_inc(down_done, 1)
                if name in ("output", "gather"):
                    half = 0 if name == "output" else 1
                    if half == 1:
                        pe.wait_ge(consts, 3)
                    for k in range(0, HTILES, 2):
                        pe.wait_ge(yts_done, HTILES // 2 * half + k // 2 + 1)
                        bank = SHARED_BANKS[k // 2]
                        pe.wait_ge(emptied[bank], uses_before_output[bank] if half == 0 else all_uses[bank])
                        if half == 1:
                            pe.wait_ge(res_ready, k // 2 + 1)
                        for t in range(k, k + 2):
                            if half == 0:
                                last = nc.tensor.transpose(banks[bank][:, tile(t - k)], yts[:, half, tile(t)], ident[:])
                            else:
                                nc.tensor.matmul(banks[bank][:, C * (t - k):C * (t - k + 1)], yts[:, half, tile(t)],
                                                 twin[:], start=(t == k), stop=False)
                        if half == 0:
                            last.then_inc(y_filled, 1)
                if name == "last experts":
                    n = UNITS - 2 + i
                    for t in range(HTILES):
                        if i == 0 and t == 0:
                            wait_hid(pe, n)
                        if i == 1 and t % 2 == 0:
                            wait_hid(pe, n, piece=t // 2)
                        last = nc.tensor.matmul(banks[SHARED_BANKS[t // 2]][:, C * (t % 2):C * (t % 2 + 1)],
                                                hid[:, n % HID, tile(t)], w3_in[:, n % EXPERTS, :],
                                                start=False, stop=(i == 1 and t % 2 == 1))
                        if i == 1 and t % 2 == 1:
                            last.then_inc(y_filled, 1)


_INS = ["x", "L0_conv_wq", "L0_conv_bq", "L0_conv_wk", "L0_conv_bk", "L0_conv_wv", "L0_conv_bv", "L0_conv_gamma",
        "L1_attn_Q", "L1_attn_E", "L1_ffn_gate_w", "L1_ffn_gate_b", "L1_ffn_w1", "L1_ffn_w2", "L1_ffn_w3"]
_OUT = ((4, 16, 16, 64), "float32")


def kernel(**inputs):
    import numpy as _np
    import concourse.bacc as _bacc
    from concourse import mybir as _mybir
    from concourse.bass_utils import run_bass_kernel_spmd as _run

    nc = _bacc.Bacc("TRN2", target_bir_lowering=False, num_devices=1)
    arrays, args = {}, []
    for name in _INS:
        a = _np.ascontiguousarray(inputs[name])
        if a.ndim == 0:
            a = a.reshape(1)
        arrays[f"in_{name}"] = a
        args.append(nc.dram_tensor(f"in_{name}", a.shape, _mybir.dt.from_np(a.dtype), kind="ExternalInput").ap())
    scratch = nc.dram_tensor("dispatch_scratch", (HALVES, EXPERTS, HALF), _mybir.dt.float32).ap()
    shape, dtype = _OUT
    out = nc.dram_tensor("out", shape, _mybir.dt.from_np(_np.dtype(dtype)), kind="ExternalOutput").ap()
    hybrid_kernel(nc, *args, scratch, out)
    result = _run(nc, [arrays], core_ids=[0])
    return result.results[0]["out"]
```
